# Optimizing a Trainium2 kernel written in Bass

```python
import numpy as np
import jax
import jax.numpy as jnp

def _softmax(x, axis=-1):
    return jax.nn.softmax(x, axis=axis)

def _gelu(x):
    return jax.nn.gelu(x, approximate=True)

def _silu(x):
    return jax.nn.silu(x)

def _sigmoid(x):
    return jax.nn.sigmoid(x)

def _layernorm(x, axis=-1, eps=1e-05):
    m = jnp.mean(x, axis=axis, keepdims=True)
    v = jnp.var(x, axis=axis, keepdims=True)
    return (x - m) / jnp.sqrt(v + eps)

def _scatter_add(tgt, idx, src, axis=0):
    return tgt.at[idx].add(src)

def _segment_sum(src, seg, n):
    return jax.ops.segment_sum(src, seg, n)
kernel_name = 'mk_xattn_ffn_d1_seqx_r8_fcc498'

def setup_inputs(seed: int=0):
    np.random.seed(seed)
    _w = jnp.asarray

    def _rec_inputs():
        import jax
        import jax.numpy as jnp
        _rk = jax.random.key(seed)
        x = 7.22e-05 + 1 * jax.random.normal(jax.random.fold_in(_rk, 1), (16, 128, 256), jnp.float32)
        _lenS = 128 - jax.random.randint(jax.random.fold_in(_rk, 7), (16,), 0, max(1, 128 // 4) + 1, jnp.int32)
        _lenS2 = 128 - jax.random.randint(jax.random.fold_in(_rk, 8), (16,), 0, max(1, 128 // 4) + 1, jnp.int32)
        _ctx_512P = jax.random.normal(jax.random.fold_in(_rk, 11), (16, 16, 64), jnp.float32)
        _ctx_512c = jax.random.dirichlet(jax.random.fold_in(_rk, 511), 0.3 * jnp.ones((16,), jnp.float32), (16, 128))
        _ctx_512t = jnp.einsum('bsk,bkd->bsd', _ctx_512c, _ctx_512P)
        _ctx_512t = _ctx_512t * jax.lax.rsqrt(jnp.mean(jnp.square(_ctx_512t)) + 1e-12) * 0.953939
        ctx_512 = -0.000514642 + 1.00011 * (_ctx_512t + 0.3 * jax.random.normal(jax.random.fold_in(_rk, 611), (16, 128, 64), jnp.float32))
        return (x, ctx_512)
    x, ctx_512 = _rec_inputs()

    def _L0_xattn_setup():
        import jax, jax.numpy as jnp
        import numpy as np
        import math
        NUM_Q_HEADS = 32
        NUM_KV_HEADS = 8
        key = jax.random.key(seed)
        k1, k2, k3 = jax.random.split(key, 3)
        B, S, E = (2, 256, 256)
        kv_E = NUM_KV_HEADS * (E // NUM_Q_HEADS)
        q = jax.random.normal(k1, (B, S, E), dtype=jnp.float32)
        k = jax.random.normal(k2, (B, S, kv_E), dtype=jnp.float32)
        v = jax.random.normal(k3, (B, S, kv_E), dtype=jnp.float32)
        return {'q': q, 'k': k, 'v': v}
    _L0_xattn_all = _L0_xattn_setup()
    _L0_xattn_in = {k: v for k, v in _L0_xattn_all.items() if k in ()}
    del _L0_xattn_all

    def _L0_ffn_setup():
        import jax, jax.numpy as jnp
        import numpy as np
        TOP_K = 6
        CAP_FACTOR = 2

        def _moe_block(x2d, wg_router, w_gate, w_up, w_down, ws_gate, ws_up, ws_down):
            T, D = x2d.shape
            E = wg_router.shape[0]
            scores = jax.nn.softmax(x2d @ wg_router.T, axis=-1)
            topk_w, topk_idx = jax.lax.top_k(scores, TOP_K)
            topk_w = topk_w / (jnp.sum(topk_w, axis=-1, keepdims=True) + 1e-20)
            flat_idx = topk_idx.reshape(-1)
            oh = jax.nn.one_hot(flat_idx, E, dtype=jnp.int32)
            pos = jnp.cumsum(oh, axis=0) - 1
            pos_in_e = jnp.take_along_axis(pos, flat_idx[:, None], axis=1)[:, 0]
            C = CAP_FACTOR * (T * TOP_K // E)
            valid = pos_in_e < C
            safe_pos = jnp.where(valid, pos_in_e, 0)
            tok_id = jnp.repeat(jnp.arange(T), TOP_K)
            vmask = valid[:, None].astype(x2d.dtype)
            x_rep = x2d[tok_id] * vmask
            xe = jnp.zeros((E, C, D), x2d.dtype).at[flat_idx, safe_pos].add(x_rep)
            g = jnp.einsum('ecd,edf->ecf', xe, w_gate)
            u = jnp.einsum('ecd,edf->ecf', xe, w_up)
            ye = jnp.einsum('ecf,efd->ecd', jax.nn.silu(g) * u, w_down)
            y_tok = ye[flat_idx, safe_pos] * vmask
            y = jnp.sum(y_tok.reshape(T, TOP_K, D) * topk_w[..., None], axis=1)
            sh = jax.nn.silu(x2d @ ws_gate) * (x2d @ ws_up) @ ws_down
            return y + sh
        key = jax.random.key(seed)
        ks = jax.random.split(key, 9)
        B, S, D, F, E = (1, 256, 256, 176, 32)
        FS = F * 2
        s = 0.02
        return {'hidden_states': jax.random.normal(ks[0], (B, S, D), jnp.float32), 'wg_router': jax.random.normal(ks[1], (E, D), jnp.float32) * s, 'w_gate': jax.random.normal(ks[2], (E, D, F), jnp.float32) * s, 'w_up': jax.random.normal(ks[3], (E, D, F), jnp.float32) * s, 'w_down': jax.random.normal(ks[4], (E, F, D), jnp.float32) * s, 'ws_gate': jax.random.normal(ks[5], (D, FS), jnp.float32) * s, 'ws_up': jax.random.normal(ks[6], (D, FS), jnp.float32) * s, 'ws_down': jax.random.normal(ks[7], (FS, D), jnp.float32) * s}
    _L0_ffn_all = _L0_ffn_setup()
    _L0_ffn_in = {k: v for k, v in _L0_ffn_all.items() if k in ('wg_router', 'w_gate', 'w_up', 'w_down', 'ws_gate', 'ws_up', 'ws_down')}
    del _L0_ffn_all
    return {'x': x, 'ctx_512': ctx_512, 'L0_ffn_wg_router': _L0_ffn_in['wg_router'], 'L0_ffn_w_gate': _L0_ffn_in['w_gate'], 'L0_ffn_w_up': _L0_ffn_in['w_up'], 'L0_ffn_w_down': _L0_ffn_in['w_down'], 'L0_ffn_ws_gate': _L0_ffn_in['ws_gate'], 'L0_ffn_ws_up': _L0_ffn_in['ws_up'], 'L0_ffn_ws_down': _L0_ffn_in['ws_down']}

def reference(x, ctx_512, L0_ffn_wg_router, L0_ffn_w_gate, L0_ffn_w_up, L0_ffn_w_down, L0_ffn_ws_gate, L0_ffn_ws_up, L0_ffn_ws_down):
    import jax
    import jax.numpy as jnp

    def _L0_xattn_ref(q, k, v):
        import jax, jax.numpy as jnp
        import numpy as np
        import math
        NUM_Q_HEADS = 32
        NUM_KV_HEADS = 8
        B, S, E = q.shape
        H, KV = (NUM_Q_HEADS, NUM_KV_HEADS)
        D = E // H
        G = H // KV
        scale = math.sqrt(D)
        qh = q.reshape(B, S, KV, G, D).transpose(0, 2, 3, 1, 4)
        kh = k.reshape(B, S, KV, D).transpose(0, 2, 1, 3)
        vh = v.reshape(B, S, KV, D).transpose(0, 2, 1, 3)
        scores = jnp.einsum('bkgsd,bktd->bkgst', qh, kh) / scale
        weights = jax.nn.softmax(scores, axis=-1)
        out = jnp.einsum('bkgst,bktd->bkgsd', weights, vh)
        return out.transpose(0, 3, 1, 2, 4).reshape(B, S, E)

    def _L0_ffn_ref(hidden_states, wg_router, w_gate, w_up, w_down, ws_gate, ws_up, ws_down):
        import jax, jax.numpy as jnp
        import numpy as np
        TOP_K = 6
        CAP_FACTOR = 2

        def _moe_block(x2d, wg_router, w_gate, w_up, w_down, ws_gate, ws_up, ws_down):
            T, D = x2d.shape
            E = wg_router.shape[0]
            scores = jax.nn.softmax(x2d @ wg_router.T, axis=-1)
            topk_w, topk_idx = jax.lax.top_k(scores, TOP_K)
            topk_w = topk_w / (jnp.sum(topk_w, axis=-1, keepdims=True) + 1e-20)
            flat_idx = topk_idx.reshape(-1)
            oh = jax.nn.one_hot(flat_idx, E, dtype=jnp.int32)
            pos = jnp.cumsum(oh, axis=0) - 1
            pos_in_e = jnp.take_along_axis(pos, flat_idx[:, None], axis=1)[:, 0]
            C = CAP_FACTOR * (T * TOP_K // E)
            valid = pos_in_e < C
            safe_pos = jnp.where(valid, pos_in_e, 0)
            tok_id = jnp.repeat(jnp.arange(T), TOP_K)
            vmask = valid[:, None].astype(x2d.dtype)
            x_rep = x2d[tok_id] * vmask
            xe = jnp.zeros((E, C, D), x2d.dtype).at[flat_idx, safe_pos].add(x_rep)
            g = jnp.einsum('ecd,edf->ecf', xe, w_gate)
            u = jnp.einsum('ecd,edf->ecf', xe, w_up)
            ye = jnp.einsum('ecf,efd->ecd', jax.nn.silu(g) * u, w_down)
            y_tok = ye[flat_idx, safe_pos] * vmask
            y = jnp.sum(y_tok.reshape(T, TOP_K, D) * topk_w[..., None], axis=1)
            sh = jax.nn.silu(x2d @ ws_gate) * (x2d @ ws_up) @ ws_down
            return y + sh
        B, S, D = hidden_states.shape
        x2d = hidden_states.reshape(-1, D)
        out = _moe_block(x2d, wg_router, w_gate, w_up, w_down, ws_gate, ws_up, ws_down)
        return out.reshape(B, S, D)
    x = x + _L0_xattn_ref(_layernorm(x, axis=-1), ctx_512, ctx_512)
    x = x + _L0_ffn_ref(_layernorm(x, axis=-1), L0_ffn_wg_router, L0_ffn_w_gate, L0_ffn_w_up, L0_ffn_w_down, L0_ffn_ws_gate, L0_ffn_ws_up, L0_ffn_ws_down)
    return x

_drawn_inputs = setup_inputs


def setup_inputs(seed=0):
    import zlib

    import numpy as np

    out = dict(_drawn_inputs(seed))
    spreads = {}
    factors = {'L0_ffn_wg_router': 8.0,
     'L0_ffn_w_gate': 8.0,
     'L0_ffn_w_up': 8.0,
     'L0_ffn_w_down': 8.0,
     'L0_ffn_ws_gate': 3.968,
     'L0_ffn_ws_up': 3.931,
     'L0_ffn_ws_down': 3.925}
    for name, (base, spread) in spreads.items():
        noise = np.random.default_rng([zlib.crc32(name.encode()), seed]).standard_normal(out[name].shape)
        drawn = base * np.exp(spread * noise) if base else spread * noise
        out[name] = jnp.asarray(drawn.astype(out[name].dtype))
    for name, factor in factors.items():
        out[name] = (out[name] * factor).astype(out[name].dtype)
    return out
```

```python
from contextlib import ExitStack

import numpy as np
import concourse.bass as bass
from concourse import mybir

F32 = mybir.dt.float32
BF16 = mybir.dt.bfloat16
U32 = mybir.dt.uint32
I32 = mybir.dt.int32
ALU = mybir.AluOpType
ACT = mybir.ActivationFunctionType
X = mybir.AxisListType.X

P = 128
B, S, D = 16, 128, 256
T = B * S
KV, G, DH = 8, 4, 8
HEADS = KV * G
NEXP, TOPK, FF = 32, 6, 176
CAP = 2 * (T * TOPK // NEXP)
CAP_BLOCKS = CAP // P
PARTS = 6
KROWS = PARTS * DH
KPAD = 64
SCALE = float(1.0 / np.sqrt(np.float32(DH)))
LN_EPS = 1e-5
NSHARED = 2
NE2 = NEXP + NSHARED
SH_TILES = NSHARED * B
MOE_TILES = (T * TOPK) // P + NEXP
TILES = SH_TILES + MOE_TILES
BLOCKS = (NEXP - 1) * CAP_BLOCKS + MOE_TILES
ROWS = BLOCKS * P
TRASH = ROWS
PADROWS = T + P
GU = 2 * FF
F0, F1 = P, FF - P


def build(nc, x, ctx, wrT, wgu, wdn0, wdn1, out):
    n2_d = nc.dram_tensor("n2_rows", (PADROWS, D), F32, kind="Internal").ap()
    acc_d = [nc.dram_tensor(f"acc{i}", (PADROWS, D), F32, kind="Internal").ap() for i in range(2)]
    tab_d = nc.dram_tensor("pair_table", (ROWS + TOPK * T, 2), F32, kind="Internal").ap()
    es = ExitStack()
    with es:
        def sb(name, shape, dt=F32):
            return es.enter_context(nc.sbuf_tensor(name, shape, dt))

        def sem(name):
            return es.enter_context(nc.semaphore(name))

        wgu_s = sb("wgu_s", [P, NE2, 2, GU])
        wdn0_s = sb("wdn0_s", [P, NE2, D])
        wdn1_s = sb("wdn1_s", [F1, NE2, D])
        wr_s = sb("wr_s", [P, 2, NEXP])
        idf = sb("idf", [P, P])
        idb = sb("idb", [P, P], BF16)
        ones = sb("ones", [P, P])
        before = sb("before", [P, P])
        kvsel = sb("kvsel", [P, KV, P], BF16)
        lane = sb("lane", [P, NEXP])
        neghalf = sb("neghalf", [P, 1])
        jcol = sb("jcol", [P, 1])
        thr = sb("thr", [P, CAP_BLOCKS])
        xq = sb("xq", [P, 2, D])
        xr = sb("xr", [P, 2, D])
        cb = sb("cb", [P, 2, KV * DH])
        hT = sb("n1_rem_or_hT", [P, 2, D])
        n1, rem = [hT[:, i, :].rearrange("p (h d) -> p h d", d=DH) for i in range(2)]
        krem = sb("krem", [P, KV, DH])
        qs = sb("qs", [P, HEADS, KPAD], BF16)
        ks = sb("ks", [P, KV, KPAD], BF16)
        vx = sb("vx", [P, 2, KV, DH + 1])
        arena = sb("qT_or_xg_yy", [P, 8, D])
        qT = arena[:, :, :].rearrange("p a d -> p (a d)").bitcast(BF16).rearrange(
            "p (u k s) -> p u k s", u=2, k=KV // 2)
        xg, yy = arena[:, 0:4, :], arena[:, 4:8, :]
        kT = sb("kT", [P, 2, KV // 2, S], BF16)
        nm = sb("nm", [P, G, KV])
        mm = sb("mm", [P, G, P], BF16)
        mT = sb("mT", [P, G * S], BF16)
        prx = sb("pr_or_xT_sg", [P, 2 * G * S])
        pr = prx[:, :].rearrange("p (u s) -> p u s", u=2)
        xT = prx[:, 0:2 * D].rearrange("p (u d) -> p u d", u=2)
        sg = prx[:, 2 * D:2 * D + 2 * FF].rearrange("p (u d) -> p u d", u=2)
        st1 = sb("st1", [P, 6])
        mv1 = sb("mv1", [P, 2])
        ve1 = sb("ve1", [P, 1])
        rs1 = sb("rs1", [P, 1])
        st2 = sb("st2", [P, 6])
        mv2 = sb("mv2", [P, 2])
        ve2 = sb("ve2", [P, 1])
        rs2 = sb("rs2", [P, 1])
        den = sb("den", [P, HEADS, 1])
        hh = sb("at_n2T_or_h", [P, 2, D])
        at = hh[:, 0, :].rearrange("p (h d) -> p h d", d=DH)
        n2T = hh[:, 1, :].rearrange("p (c t) -> p c t", c=2)
        x2 = sb("x2", [P, 2, D])
        n2 = sb("n2", [P, 2, D])
        nlm = sb("nlm", [P, 1])
        pe_ = sb("pe_", [P, NEXP])
        zs = sb("zs", [P, 1])
        rz = sb("rz", [P, 1])
        sc = sb("sc", [P, NEXP])
        top = sb("top", [P, 8])
        tix = sb("tix", [P, 8], U32)
        s6 = sb("s6", [P, 1])
        s6e = sb("s6e", [P, 1])
        r6 = sb("r6", [P, 1])
        ixf = sb("ixf", [P, TOPK, 1])
        oh = sb("oh", [P, TOPK, NEXP])
        mk = sb("mk", [P, NEXP])
        run = sb("run", [P, 2, NEXP])
        pp = sb("pp", [P, TOPK, NEXP])
        pk = sb("pk", [P, TOPK])
        va = sb("va", [P, TOPK])
        sl0 = sb("sl0", [P, TOPK])
        sl1 = sb("sl1", [P, TOPK])
        sl2 = sb("sl2", [P, TOPK])
        tok = sb("tok", [P, 1])
        trc = sb("trc", [P, TOPK])
        slot = sb("slot", [P, 2, TOPK], U32)
        dat = sb("dat", [P, 2, TOPK, 2])
        etab = sb("etab", [1, TILES + 8], I32)
        idsT = sb("idsT", [P, TILES + 8])
        wT = sb("wT", [P, TILES + 8])
        ixg = sb("ixg", [P, 2, 4], U32)
        ixa = sb("ixa", [P, 2, 4], U32)
        wj = sb("wj", [P, 2, 4])
        init = xg.rearrange("p a d -> p (a d)")[:, 0:2 * BLOCKS].rearrange(
            "p (r c) -> p r c", c=2)
        initi = yy.rearrange("p a d -> p (a d)")[:, 0:BLOCKS].bitcast(I32)
        zero = yy[:, 2, :]
        blk = sb("blk", [P, 1], U32)
        ej = sb("ej", [P, 1])
        toj = sb("toj", [P, 1])
        jr = sb("jr", [P, 1])
        cum = sb("cum", [P, NEXP])
        ntl = sb("ntl", [P, NEXP])
        cc = sb("cc", [P, NEXP])
        le = sb("le", [P, NEXP])
        lec = sb("lec", [P, NEXP])
        g2 = x2[:, 0, :].rearrange("p (r c) -> p r c", c=2)
        FCH = 4
        wflat = wgu_s[:, :, :, :].rearrange("p e c f -> p (e c f)")
        fa, fb = [wflat[:, i * B * D:(i + 1) * B * D].rearrange("p (c a d) -> p c a d", c=FCH, d=D)
                  for i in range(2)]

        ps = es.enter_context(nc.psum_tensor("ps", [P, 8, 512], F32))
        psb = ps[:, :, :].bitcast(BF16)
        SM, SE, CQ, OB, DB = 0, 2, 4, 6, 7
        XB, LB, GB, HB, YB = 0, 1, 2, 4, 6

        names = """held const_pool const_dve init_iota init_and init_add init_zero init_done wr_in w_in
        kc0 kc1 kc2 kc3 ks_ready vx_ready stat1 mean1 veps1 rstd1 n1_ready qcopy0 qrem qcopy1 qs_ready
        q_tr k_tr m_tr q_ev k_ev m_ev s1 s2 pv rowmax mm_hi mm_ready expd
        den_ready o_free x2_ready stat2 mean2 veps2 rstd2 n2_ready n2_tr n2_ev lg lgmax pexp
        rz_ready sc_ready top_ready tix_ready s6_ready s6e_ready r6_ready w_ready ixf_ready
        oh_ready mk_ready run_ready pos pp_ready pk_ready va_ready sl0_ready sl1_ready sl2_ready slot_ready ids_ready
        tok_ready cnt cc_ready gt_ready nt_ready cum_ready le_ready ej_ready lec_ready toj_ready jr_ready
        blk_ready h_pad g2_in et_mm et_ready idt_tr ids_all wt_all
        ixg_ready ixa_ready x_tr xT_ready gu sg_ready h_ready h_tr hT_ready dn y_ready
        fin_add fin_done""".split()
        sig = {n: sem(n) for n in names}
        xq_in = [sem(f"xq_in{i}") for i in range(2)]
        xr_in = [sem(f"xr_in{i}") for i in range(2)]
        c_in = [sem(f"c_in{i}") for i in range(2)]
        x2_st = [sem(f"x2_st{i}") for i in range(2)]
        n2_st = [sem(f"n2_st{i}") for i in range(2)]
        pair_st = [sem(f"pair_st{i}") for i in range(2)]
        g_in = [sem(f"g_in{i}") for i in range(4)]
        y_st = [sem(f"y_st{i}") for i in range(4)]
        f_in = [sem(f"f_in{i}") for i in range(FCH)]
        f_st = sem("f_st")
        NCONST_POOL, NCONST_DVE = 13, 13

        block = es.enter_context(nc.Block())

        def due(n):
            return not isinstance(n, int) or n > 0

        def settle(eng):
            eng.sem_inc(sig["held"], 1)

        def steps(eng, step):
            for b in (-2, -1, 0, 1):
                step(b, b // 2, b % 2)
            with eng.Fori(1, B // 2 - 1) as h:
                for u in range(2):
                    step(2 * h + u, h, u)
            for b in (B - 2, B - 1, B):
                step(b, b // 2, b % 2)

        def has(b, off):
            return not isinstance(b, int) or 0 <= b + off < B

        AHEAD = 4

        def eights(eng, tile):
            for r in range(8):
                tile(r, 0, r)
            with eng.Fori(1, TILES // 8 - 1) as m:
                for r in range(8):
                    tile(8 * m + r, m, r)
            for r in range(8):
                tile(TILES - 8 + r, TILES // 8 - 1, r)

        @block.sync
        def _(sp):
            def load_q(b, h, u):
                sp.dma_start(xq[:, u, :], x[bass.ds(b, 1), :, :].rearrange("a p d -> p (a d)")).then_inc(xq_in[u], 16)
                sp.dma_start(cb[:, u, :], ctx[bass.ds(b, 1), :, :].rearrange("a p d -> p (a d)")).then_inc(c_in[u], 16)

            def load_r(b, u):
                sp.dma_start(xr[:, u, :], x[bass.ds(b, 1), :, :].rearrange("a p d -> p (a d)")).then_inc(xr_in[u], 16)

            load_q(0, 0, 0)
            load_q(1, 0, 1)
            sp.dma_start(wr_s[:, :, :], wrT).then_inc(sig["wr_in"], 16)
            sp.wait_ge(sig["init_zero"], 1)
            for i in range(B + 1):
                sp.dma_start(acc_d[1][i * P:(i + 1) * P, :], zero).then_inc(sig["init_done"], 16)
            sp.dma_start(acc_d[0][T:PADROWS, :], zero).then_inc(sig["init_done"], 16)
            sp.dma_start(n2_d[T:PADROWS, :], zero).then_inc(sig["init_done"], 16)
            sp.wait_ge(sig["init_add"], 2)
            sp.dma_start(tab_d[0:ROWS, :].rearrange("(p r) c -> p r c", p=P), init).then_inc(sig["init_done"], 16)

            def step(b, h, u):
                o = 1 - u
                if has(b, -1):
                    if due(b):
                        sp.wait_ge(sig["x2_ready"], b)
                    sp.dma_start(acc_d[0][bass.ds((b - 1) * P, P), :], x2[:, o, :]).then_inc(x2_st[o], 16)
                if has(b, 1):
                    load_r(b + 1, o)
                if has(b, -1):
                    if due(b):
                        sp.wait_ge(sig["n2_ready"], b)
                    sp.dma_start(n2_d[bass.ds((b - 1) * P, P), :], n2[:, o, :]).then_inc(n2_st[o], 16)
                if has(b, 0):
                    e = 2 * b
                    sp.dma_start(wgu_s[:, bass.ds(e, 2), :, :], wgu[:, bass.ds(e, 2), :, :]).then_inc(sig["w_in"], 16)
                    sp.dma_start(wdn0_s[:, bass.ds(e, 2), :], wdn0[:, bass.ds(e, 2), :]).then_inc(sig["w_in"], 16)
                    sp.dma_start(wdn1_s[:, bass.ds(e, 2), :], wdn1[:, bass.ds(e, 2), :]).then_inc(sig["w_in"], 16)
                if has(b, 4):
                    sp.wait_ge(sig["n1_ready"], b + 3)
                    sp.wait_ge(sig["vx_ready"], b + 3)
                    load_q(b + 4, h, u)

            for b in (-2, -1, 0, 1):
                step(b, b // 2, b % 2)
            with sp.Fori(1, B // 2 - 2) as h:
                for u in range(2):
                    step(2 * h + u, h, u)
            for b in range(B - 4, B + 1):
                step(b, b // 2, b % 2)
            e = NEXP
            sp.dma_start(wgu_s[:, e:, :, :], wgu[:, e:, :, :]).then_inc(sig["w_in"], 16)
            sp.dma_start(wdn0_s[:, e:, :], wdn0[:, e:, :]).then_inc(sig["w_in"], 16)
            sp.dma_start(wdn1_s[:, e:, :], wdn1[:, e:, :]).then_inc(sig["w_in"], 16)

            for i in range(4):
                sp.wait_ge(y_st[i], 16 * (TILES // 4))
            fv = [a[0:T, :].rearrange("(c a p) d -> c p a d", p=P, c=FCH) for a in acc_d]
            ov = out.rearrange("(c a) p d -> c p a d", c=FCH)
            for c in range(FCH):
                sp.dma_start(fa[:, c, :, :], fv[0][c]).then_inc(f_in[c], 16)
                sp.dma_start(fb[:, c, :, :], fv[1][c]).then_inc(f_in[c], 16)
            for c in range(FCH):
                sp.wait_ge(sig["fin_add"], c + 1)
                sp.dma_start(ov[c], fa[:, c, :, :]).then_inc(f_st, 16)
            sp.wait_ge(f_st, 16 * FCH)

        @block.gpsimd
        def _(pool):
            g = nc.gpsimd
            cp = sig["const_pool"]
            g.memset(idf[:, :], 0.0).then_inc(cp, 1)
            g.memset(idb[:, :], 0.0).then_inc(cp, 1)
            g.memset(before[:, :], 1.0).then_inc(cp, 1)
            g.memset(kvsel[:, :, :], 1.0).then_inc(cp, 1)
            g.iota(initi, [[1, BLOCKS]], base=0, channel_multiplier=BLOCKS % P).then_inc(sig["init_iota"], 1)
            pool.wait_ge(cp, 4)
            for m in (idf, idb):
                g.affine_select(out=m[:, :], in_=m[:, :], compare_op=ALU.not_equal, fill=1.0, base=0,
                                pattern=[[-1, P]], channel_multiplier=1).then_inc(cp, 1)
            g.affine_select(out=before[:, :], in_=before[:, :], compare_op=ALU.is_gt, fill=0.0, base=0,
                            pattern=[[1, P]], channel_multiplier=-1).then_inc(cp, 1)
            ksv = kvsel[:, :, :].rearrange("p (a b) c -> p a b c", b=2)
            g.affine_select(out=ksv, in_=ksv, compare_op=ALU.is_ge, fill=0.0, base=0,
                            pattern=[[-2, KV // 2], [-KPAD, 2], [0, P]], channel_multiplier=1).then_inc(cp, 1)
            pool.wait_ge(cp, 8)
            g.affine_select(out=ksv, in_=ksv, compare_op=ALU.is_ge, fill=0.0, base=1,
                            pattern=[[2, KV // 2], [KPAD, 2], [0, P]], channel_multiplier=-1).then_inc(cp, 1)
            g.iota(lane[:, :], [[1, NEXP]], base=0, channel_multiplier=0, allow_small_or_imprecise_dtypes=True)
            g.iota(jcol[:, :], [[1, 1]], base=0, channel_multiplier=1, allow_small_or_imprecise_dtypes=True)
            g.iota(thr[:, :], [[P, CAP_BLOCKS]], base=0, channel_multiplier=0, allow_small_or_imprecise_dtypes=True)
            g.iota(tok[:, :], [[1, 1]], base=0, channel_multiplier=1, allow_small_or_imprecise_dtypes=True)
            g.iota(trc[:, :], [[T, TOPK]], base=TRASH, channel_multiplier=1, allow_small_or_imprecise_dtypes=True)
            g.iota(etab[0:1, 0:SH_TILES], [[0, B], [1, NSHARED]], base=NEXP, channel_multiplier=0)
            g.iota(idsT[:, 0:SH_TILES], [[P, B], [0, NSHARED]], base=0, channel_multiplier=1,
                   allow_small_or_imprecise_dtypes=True)
            g.memset(neghalf[:, :], -0.5)
            g.memset(wT[:, 0:SH_TILES], 1.0)
            g.memset(vx[:, :, :, DH:DH + 1], 1.0).then_inc(cp, 4)

            def rstd(var, veps, dst, s0, s1, b):
                settle(pool)
                g.tensor_scalar(veps[:, :], var, LN_EPS, None, ALU.add).then_inc(s0, 1)
                if due(b + 1):
                    pool.wait_ge(s0, b + 1)
                g.tensor_tensor(dst[:, :], veps[:, :], neghalf[:, :], ALU.pow).then_inc(s1, 1)

            def step(b, h, u):
                o = 1 - u
                if has(b, -1):
                    if due(b):
                        pool.wait_ge(sig["mean2"], b)
                    rstd(mv2[:, 1:2], ve2, rs2, sig["veps2"], sig["rstd2"], b - 1)
                if has(b, 2):
                    n = b + 2
                    if due(n + 1):
                        pool.wait_ge(sig["mean1"], n + 1)
                    if has(b, 1):
                        if due(n):
                            pool.wait_ge(sig["n1_ready"], n)
                    rstd(mv1[:, 1:2], ve1, rs1, sig["veps1"], sig["rstd1"], n)
                    if due(16 * (h + 2)):
                        pool.wait_ge(c_in[u], 16 * (h + 2))
                    if due(n):
                        pool.wait_ge(sig["k_tr"], n)
                    c3 = cb[:, u, :].rearrange("p (k d) -> p k d", d=DH)
                    kv4 = ks[:, :, 0:KROWS].rearrange("p k (j d) -> p k j d", d=DH)
                    kj = [kv4[:, :, j, :] for j in range(PARTS)]
                    settle(pool)
                    g.tensor_copy(kj[0], c3).then_inc(sig["kc0"], 1)
                    g.tensor_copy(kj[3], c3)
                    g.tensor_copy(kj[5], c3)
                    if due(n + 1):
                        pool.wait_ge(sig["kc0"], n + 1)
                    g.tensor_tensor(krem[:, :, :], c3, kj[0], ALU.subtract).then_inc(sig["kc1"], 1)
                    if due(n + 1):
                        pool.wait_ge(sig["kc1"], n + 1)
                    settle(pool)
                    g.tensor_copy(kj[1], krem[:, :, :]).then_inc(sig["kc2"], 1)
                    g.tensor_copy(kj[4], krem[:, :, :])
                    if due(n + 1):
                        pool.wait_ge(sig["kc2"], n + 1)
                    g.tensor_tensor(kj[2], krem[:, :, :], kj[1], ALU.subtract).then_inc(sig["ks_ready"], 1)
                if has(b, -1):
                    if due(b):
                        pool.wait_ge(sig["slot_ready"], b)
                    if due(b):
                        pool.wait_ge(sig["ids_ready"], b)
                    if due(b):
                        pool.wait_ge(sig["w_ready"], b)
                    if isinstance(b, int) and b == 1:
                        pool.wait_ge(sig["init_done"], 16 * (B + 4))
                    settle(pool)
                    for k in range(TOPK):
                        g.indirect_dma_start(tab_d, bass.IndirectOffsetOnAxis(ap=slot[:, o, k:k + 1], axis=0),
                                             dat[:, o, k, :], None).then_inc(pair_st[o], 16)
                if has(b, 2):
                    if has(b, 0):
                        if due(KV * b + KV):
                            pool.wait_ge(sig["pv"], KV * b + KV)
                        settle(pool)
                    g.tensor_copy(vx[:, u, :, 0:DH], cb[:, u, :].rearrange("p (k d) -> p k d", d=DH)
                                  ).then_inc(sig["vx_ready"], 1)

            steps(pool, step)

            def gather(j, m, r):
                if r % 4 == 0:
                    pool.wait_ge(sig["ixg_ready"], 2 * m + r // 4 + 1)
                if not isinstance(j, int) or j >= 4:
                    pool.wait_ge(sig["x_tr"], j - 3)
                settle(pool)
                g.indirect_dma_start(xg[:, r % 4, :], None, n2_d,
                                     bass.IndirectOffsetOnAxis(ap=ixg[:, r // 4, r % 4:r % 4 + 1], axis=0)
                                     ).then_inc(g_in[r % 4], 16)

            def add(j, m, r):
                pool.wait_ge(sig["y_ready"], j + 1)
                if r % 4 == 0:
                    pool.wait_ge(sig["ixa_ready"], 4 * m + 2 * (r // 4) + 2)
                if r >= 2:
                    pool.wait_ge(y_st[(r - 2) % 4], 32 * m + 16 * ((r - 2) // 4 + 1))
                elif not isinstance(m, int) or m > 0:
                    pool.wait_ge(y_st[r + 2], 32 * m)
                settle(pool)
                g.indirect_dma_start(acc_d[r % 2], bass.IndirectOffsetOnAxis(ap=ixa[:, r // 4, r % 4:r % 4 + 1], axis=0),
                                     yy[:, r % 4, :], None, compute_op=ALU.add).then_inc(y_st[r % 4], 16)

            for i in range(2):
                pool.wait_ge(n2_st[i], 16 * (B // 2))
                pool.wait_ge(x2_st[i], 16 * (B // 2))
            for j in range(AHEAD):
                gather(j, 0, j)
            pool.wait_ge(sig["blk_ready"], 1)
            for i in range(2):
                pool.wait_ge(pair_st[i], 16 * TOPK * (B // 2))
            g.indirect_dma_start(x2[:, 0, :], None, tab_d[0:ROWS, :].rearrange("(b r) c -> b (r c)", r=P),
                                 bass.IndirectOffsetOnAxis(ap=blk[:, :], axis=0)).then_inc(sig["g2_in"], 16)

            def tile(j, m, r):
                if not isinstance(j, int) or j + AHEAD < TILES:
                    gather(j + AHEAD, m + (r + AHEAD) // 8, (r + AHEAD) % 8)
                add(j, m, r)
            eights(pool, tile)

        @block.scalar
        def _(act):
            a = nc.scalar

            def step(b, h, u):
                o = 1 - u
                if has(b, 0):
                    if due(b + 1):
                        act.wait_ge(sig["m_tr"], b + 1)
                    if due(KV * b):
                        act.wait_ge(sig["s2"], KV * b)
                    a.activation(mT[:, :], psb[:, DB, 0:G * S], ACT.Copy).then_inc(sig["m_ev"], 1)
                for kv in range(KV):
                    if kv == 1 and has(b, -1):
                        if due(b):
                            act.wait_ge(sig["n2_tr"], b)
                        if due(b - 1):
                            act.wait_ge(sig["lg"], b - 1)
                        a.activation(n2T[:, :, :], ps[:, DB, 0:D], ACT.Copy).then_inc(sig["n2_ev"], 1)
                    if kv == 1 and has(b, 2):
                        if due(b + 3):
                            act.wait_ge(sig["n1_ready"], b + 3)
                        if due(2 * (b + 2)):
                            act.wait_ge(sig["q_tr"], 2 * (b + 2))
                        a.activation(qs[:, :, 0:3 * DH].rearrange("p h (j d) -> p h j d", d=DH),
                                     n1.unsqueeze(2).broadcast_to([P, HEADS, 3, DH]),
                                     ACT.Copy).then_inc(sig["qcopy0"], 1)
                    if kv == 3 and has(b, 2):
                        if due(b + 3):
                            act.wait_ge(sig["qrem"], b + 3)
                        a.activation(qs[:, :, 3 * DH:5 * DH].rearrange("p h (j d) -> p h j d", d=DH),
                                     rem.unsqueeze(2).broadcast_to([P, HEADS, 2, DH]),
                                     ACT.Copy).then_inc(sig["qcopy1"], 1)
                    if kv == 4 and has(b, -1):
                        if due(b):
                            act.wait_ge(sig["lgmax"], b)
                        a.activation(pe_[:, :], ps[:, DB, 0:NEXP], ACT.Exp, bias=nlm[:, :],
                                     accum_out=zs[:, :]).then_inc(sig["pexp"], 1)
                    if has(b, 0):
                        n = KV * b + kv
                        if due(n + 1):
                            act.wait_ge(sig["s2"], n + 1)
                        if due(n - 1):
                            act.wait_ge(sig["pv"], n - 1)
                        a.activation(pr[:, kv % 2, :], ps[:, SE + kv % 2, :], ACT.Exp,
                                     scale=SCALE).then_inc(sig["expd"], 1)
                    if kv == 6 and has(b, 2):
                        if due(2 * (b + 2) + 1):
                            act.wait_ge(sig["q_tr"], 2 * (b + 2) + 1)
                        if isinstance(b, int) and b == -2:
                            act.wait_ge(sig["init_done"], 16 * (B + 4))
                        if due(KV * b + 4):
                            act.wait_ge(sig["s2"], KV * b + 4)
                        a.activation(qT[:, u, 0:2, :], psb[:, CQ, :], ACT.Copy).then_inc(sig["q_ev"], 1)
                if has(b, 2):
                    if due(b + 3):
                        act.wait_ge(sig["k_tr"], b + 3)
                    if due(KV * b + KV):
                        act.wait_ge(sig["s2"], KV * b + KV)
                    if isinstance(b, int) and b == -2:
                        act.wait_ge(sig["init_done"], 16 * (B + 4))
                    a.activation(kT[:, u, :, :], psb[:, DB, 0:KV // 2 * S], ACT.Copy).then_inc(sig["k_ev"], 1)
                    if due(2 * (b + 2) + 2):
                        act.wait_ge(sig["q_tr"], 2 * (b + 2) + 2)
                    a.activation(qT[:, u, 2:4, :], psb[:, CQ + 1, :], ACT.Copy).then_inc(sig["q_ev"], 1)

            steps(act, step)

            def scaled(j, m, r):
                act.wait_ge(sig["dn"], j + 1)
                if r % 4 == 0:
                    act.wait_ge(sig["ixa_ready"], 4 * m + 2 * (r // 4) + 2)
                if not isinstance(j, int) or j >= 4:
                    act.wait_ge(y_st[r % 4], 32 * m + 16 * (r // 4))
                a.activation(yy[:, r % 4, :], ps[:, YB + r % 2, 0:D], ACT.Copy,
                             scale=wj[:, r // 4, r % 4:r % 4 + 1]).then_inc(sig["y_ready"], 1)

            def silu(j, r):
                w = r % 2
                act.wait_ge(sig["gu"], j + 1)
                if not isinstance(j, int) or j >= 2:
                    act.wait_ge(sig["h_ready"], j - 1)
                a.activation(sg[:, w, :], ps[:, GB + w, 0:FF], ACT.Silu).then_inc(sig["sg_ready"], 1)

            def tile(j, m, r):
                w = r % 2
                act.wait_ge(sig["h_tr"], j + 1)
                if not isinstance(j, int) or j >= 2:
                    act.wait_ge(sig["dn"], j - 1)
                a.activation(hT[:, w, :], ps[:, HB + w, 0:D], ACT.Copy).then_inc(sig["hT_ready"], 1)
                if not isinstance(j, int) or j + 1 < TILES:
                    silu(j + 1, r + 1)
                scaled(j, m, r)
            silu(0, 0)
            eights(act, tile)

        @block.tensor
        def _(pe):
            t = nc.tensor
            pe.wait_ge(sig["const_pool"], NCONST_POOL)
            pe.wait_ge(sig["const_dve"], 1)

            def q_transposes(b, half):
                for pr_ in range(2):
                    for g in range(G):
                        pair = 2 * half + pr_
                        h0 = g * KV + 2 * pair
                        last = t.transpose(psb[:, CQ + half, (pr_ * G + g) * S:(pr_ * G + g + 1) * S],
                                           qs[:, h0:h0 + 2, :].rearrange("p h k -> p (h k)"), idb[:, :])
                last.then_inc(sig["q_tr"], 1)

            def step(b, h, u):
                o = 1 - u
                if has(b, 0):
                    if due(b + 1):
                        pe.wait_ge(sig["mm_ready"], b + 1)
                    if due(b + 2 if has(b, 1) else B):
                        pe.wait_ge(sig["k_ev"], b + 2 if has(b, 1) else B)
                    for g in range(G):
                        last = t.transpose(psb[:, DB, g * S:(g + 1) * S], mm[:, g, :], idb[:, :])
                    last.then_inc(sig["m_tr"], 1)
                for kv in range(KV):
                    p0, pair = KPAD * (kv % 2), kv // 2
                    if has(b, 0):
                        n = KV * b + kv
                        if due(n - 1):
                            pe.wait_ge(sig["expd"], n - 1)
                        if kv == 0:
                            if due(b + 1):
                                pe.wait_ge(sig["m_ev"], b + 1)
                        t.matmul(ps[:, SE + kv % 2, :], kT[p0:p0 + KROWS, u, pair, :], qT[p0:p0 + KROWS, u, pair, :],
                                 start=True, stop=False)
                        t.matmul(ps[:, SE + kv % 2, :], kvsel[p0:p0 + KPAD, kv, :], mT[p0:p0 + KPAD, :],
                                 start=False, stop=True).then_inc(sig["s2"], 1)
                    if has(b, 1):
                        n = KV * (b + 1) + kv
                        if due(n - 1):
                            pe.wait_ge(sig["rowmax"], n - 1)
                        if kv == 0:
                            if due(b + 2):
                                pe.wait_ge(sig["k_ev"], b + 2)
                            if due(2 * (b + 1) + 2):
                                pe.wait_ge(sig["q_ev"], 2 * (b + 1) + 2)
                        for g in range(G):
                            last = t.matmul(ps[:, SM + kv % 2, g * S:(g + 1) * S],
                                            qT[p0:p0 + KROWS, o, pair, g * S:(g + 1) * S],
                                            kT[p0:p0 + KROWS, o, pair, :], start=True, stop=True)
                        last.then_inc(sig["s1"], 1)
                    if has(b, 0) and kv >= 1:
                        pv(b, kv - 1, u)
                    if has(b, -1):
                        if kv == 1:
                            if due(b):
                                pe.wait_ge(sig["n2_ready"], b)
                            if due(b + 1 if has(b, 0) else B):
                                pe.wait_ge(sig["m_ev"], b + 1 if has(b, 0) else B)
                            if due(b + 2 if has(b, 1) else B):
                                pe.wait_ge(sig["k_ev"], b + 2 if has(b, 1) else B)
                            for c in range(2):
                                last = t.transpose(ps[:, DB, c * P:(c + 1) * P], n2[:, o, c * P:(c + 1) * P], idf[:, :])
                            last.then_inc(sig["n2_tr"], 1)
                        if kv == 3:
                            if due(b):
                                pe.wait_ge(sig["n2_ev"], b)
                            pe.wait_ge(sig["wr_in"], 16)
                            for c in range(2):
                                last = t.matmul(ps[:, DB, 0:NEXP], n2T[:, c, :], wr_s[:, c, :],
                                                start=(c == 0), stop=(c == 1))
                            last.then_inc(sig["lg"], 1)
                        if kv == 6:
                            if due(b):
                                pe.wait_ge(sig["pexp"], b)
                            if due(b):
                                pe.wait_ge(sig["mk_ready"], b)
                            t.matmul(ps[:, DB, 0:NEXP], before[:, :], mk[:, :], start=True, stop=False)
                            t.matmul(ps[:, DB, 0:NEXP], ones[:, :], run[:, o, :],
                                     start=False, stop=True).then_inc(sig["pos"], 1)
                    if kv == 5 and has(b, 2):
                        if due(b + 3):
                            pe.wait_ge(sig["qs_ready"], b + 3)
                        if due(2 * (b + 2) - 1):
                            pe.wait_ge(sig["q_ev"], 2 * (b + 2) - 1)
                        q_transposes(b + 2, 0)
                if has(b, 2):
                    if due(2 * (b + 2)):
                        pe.wait_ge(sig["q_ev"], 2 * (b + 2))
                    q_transposes(b + 2, 1)
                    if due(b + 3):
                        pe.wait_ge(sig["ks_ready"], b + 3)
                    if due(b):
                        pe.wait_ge(sig["pp_ready"], b)
                    for pair in range(KV // 2):
                        last = t.transpose(psb[:, DB, pair * S:(pair + 1) * S],
                                           ks[:, 2 * pair:2 * pair + 2, :].rearrange("p h k -> p (h k)"), idb[:, :])
                    last.then_inc(sig["k_tr"], 1)
                if has(b, 0):
                    pv(b, KV - 1, u)

            def pv(b, kv, u):
                if due(KV * b + kv + 1):
                    pe.wait_ge(sig["expd"], KV * b + kv + 1)
                if kv == 0:
                    if due(b):
                        pe.wait_ge(sig["o_free"], b)
                    if due(b + 1):
                        pe.wait_ge(sig["vx_ready"], b + 1)
                for g in range(G):
                    c0 = (kv * G + g) * (DH + 1)
                    last = t.matmul(ps[:, OB, c0:c0 + DH + 1], pr[:, kv % 2, g * S:(g + 1) * S], vx[:, u, kv, :],
                                    start=True, stop=True)
                last.then_inc(sig["pv"], 1)

            steps(pe, step)

            def tile_list(i):
                if i == 0:
                    t.matmul(ps[:, LB, 0:NEXP], ones[:, :], run[:, 0, :], start=True, stop=True).then_inc(sig["cnt"], 1)
                if i == 2:
                    pe.wait_ge(sig["ej_ready"], 1)
                    t.matmul(ps[0:1, LB, 0:P], ej[:, :], idf[:, :], start=True, stop=True).then_inc(sig["et_mm"], 1)
                if i == 4:
                    pe.wait_ge(sig["et_ready"], 1)
                    pe.wait_ge(sig["g2_in"], 16)
                    for c in range(2):
                        last = t.transpose(ps[:, LB, c * P:(c + 1) * P], g2[:, :, c], idf[:, :])
                    last.then_inc(sig["idt_tr"], 1)

            def x_transpose(j, m, r):
                pe.wait_ge(g_in[r % 4], 32 * m + 16 * (r // 4 + 1))
                for c in range(2):
                    last = t.transpose(ps[:, XB, c * P:(c + 1) * P], xg[:, r % 4, c * P:(c + 1) * P], idf[:, :])
                last.then_inc(sig["x_tr"], 1)

            def expert_of(j):
                return nc.values_load(etab[0:1, bass.ds(j, 1)], engines=(mybir.EngineType.PE,), min_val=0, max_val=NE2 - 1,
                                      skip_runtime_bounds_check_because="a sum of 31 comparisons, or one of the shared halves")

            def gate_up(j, r, e):
                w = r % 2
                pe.wait_ge(sig["xT_ready"], j + 1)
                for c in range(2):
                    last = t.matmul(ps[:, GB + w, 0:GU], xT[:, w, c * P:(c + 1) * P],
                                    wgu_s[:, bass.ds(e, 1), c, :].rearrange("p a f -> p (a f)"),
                                    start=(c == 0), stop=(c == 1))
                last.then_inc(sig["gu"], 1)

            def h_transpose(j, r):
                w = r % 2
                pe.wait_ge(sig["h_ready"], j + 1)
                for c in range(2):
                    last = t.transpose(ps[:, HB + w, c * P:(c + 1) * P], hh[:, w, c * P:(c + 1) * P], idf[:, :])
                last.then_inc(sig["h_tr"], 1)

            def down(j, r, e):
                w = r % 2
                pe.wait_ge(sig["hT_ready"], j + 1)
                t.matmul(ps[:, YB + w, 0:D], hT[:, w, 0:P],
                         wdn0_s[:, bass.ds(e, 1), :].rearrange("p a f -> p (a f)"), start=True, stop=False)
                t.matmul(ps[:, YB + w, 0:D], hT[0:F1, w, P:2 * P],
                         wdn1_s[:, bass.ds(e, 1), :].rearrange("p a f -> p (a f)"),
                         start=False, stop=True).then_inc(sig["dn"], 1)

            pe.wait_ge(sig["w_in"], 16 * 3 * (NE2 // 2))
            x_transpose(0, 0, 0)
            pe.wait_ge(sig["xT_ready"], 1)
            x_transpose(1, 0, 1)
            gate_up(0, 0, NEXP)
            pe.wait_ge(sig["run_ready"], B)
            pe.wait_ge(sig["pp_ready"], B)
            pe.wait_ge(sig["h_pad"], 1)

            expert = {}

            def tile(j, m, r):
                if isinstance(j, int):
                    tile_list(j)
                if r == 0:
                    expert[0] = expert_of(j)
                last_one = isinstance(j, int) and j + 1 == TILES
                if not last_one:
                    expert[1] = expert_of(j + 1)
                h_transpose(j, r)
                if not last_one:
                    gate_up(j + 1, r + 1, expert[1])
                if not isinstance(j, int) or j + 2 < TILES:
                    x_transpose(j + 2, m + (r + 2) // 8, (r + 2) % 8)
                down(j, r, expert[0])
                expert[0] = expert[1]
            eights(pe, tile)

        @block.vector
        def _(dve):
            v = nc.vector
            v.memset(zero, 0.0).then_inc(sig["init_zero"], 1)
            v.memset(ones[:, :], 1.0)
            v.memset(qs[:, :, :], 0.0)
            v.memset(ks[:, :, :], 0.0)
            v.memset(mm[:, :, :], 0.0)
            v.memset(run[:, 0, :], 0.0).then_inc(sig["const_dve"], 1)
            v.memset(init[:, :, 1:2], 0.0).then_inc(sig["init_add"], 1)
            dve.wait_ge(sig["init_iota"], 1)
            v.tensor_scalar(initi, initi, P - 1, None, ALU.bitwise_and).then_inc(sig["init_and"], 1)
            dve.wait_ge(sig["init_and"], 1)
            v.tensor_scalar(init[:, :, 0:1].rearrange("p r c -> p (r c)"), initi, float(T), None,
                            ALU.add).then_inc(sig["init_add"], 1)
            dve.wait_ge(sig["const_pool"], NCONST_POOL)

            def step(b, h, u):
                o = 1 - u

                def rowmax(kv):
                    if has(b, 1):
                        n = KV * (b + 1) + kv
                        if due(n + 1):
                            dve.wait_ge(sig["s1"], n + 1)
                        if kv == 0:
                            if due(b + 1):
                                dve.wait_ge(sig["mm_ready"], b + 1)
                        v.tensor_reduce(nm[:, :, kv], ps[:, SM + kv % 2, :].rearrange("p (g t) -> p g t", g=G),
                                        X, ALU.max, negate=True).then_inc(sig["rowmax"], 1)

                if has(b, -1):
                    c = b - 1
                    if due(KV * b):
                        dve.wait_ge(sig["pv"], KV * b)
                    O = ps[:, OB, 0:HEADS * (DH + 1)].rearrange("p (h d) -> p h d", d=DH + 1)
                    v.reciprocal(den[:, :, :], O[:, :, DH:DH + 1]).then_inc(sig["den_ready"], 1)
                    if due(c + 1):
                        dve.wait_ge(sig["den_ready"], c + 1)
                    v.tensor_tensor(at[:, :, :], O[:, :, 0:DH], den[:, :, :].broadcast_to([P, HEADS, DH]),
                                    ALU.mult).then_inc(sig["o_free"], 1)
                    if due(c + 1):
                        dve.wait_ge(sig["o_free"], c + 1)
                    if due(16 * (h + u)):
                        dve.wait_ge(xr_in[o], 16 * (h + u))
                    if due(16 * (h + u - 1)):
                        dve.wait_ge(x2_st[o], 16 * (h + u - 1))
                    v.tensor_tensor(x2[:, o, :], at[:, :, :].rearrange("p h d -> p (h d)"), xr[:, o, :],
                                    ALU.add).then_inc(sig["x2_ready"], 1)
                rowmax(0)
                if has(b, -1):
                    if due(c + 1):
                        dve.wait_ge(sig["x2_ready"], c + 1)
                    v.bn_stats(st2[:, :], x2[:, o, :]).then_inc(sig["stat2"], 1)
                    if due(c + 1):
                        dve.wait_ge(sig["stat2"], c + 1)
                    settle(dve)
                    v.bn_aggr(mv2[:, :], st2[:, :]).then_inc(sig["mean2"], 1)
                if has(b, 2):
                    n = b + 2
                    if due(16 * (h + 2)):
                        dve.wait_ge(xq_in[u], 16 * (h + 2))
                    v.bn_stats(st1[:, :], xq[:, u, :]).then_inc(sig["stat1"], 1)
                    if due(n + 1):
                        dve.wait_ge(sig["stat1"], n + 1)
                    settle(dve)
                    v.bn_aggr(mv1[:, :], st1[:, :]).then_inc(sig["mean1"], 1)
                if has(b, -1):
                    if due(c + 1):
                        dve.wait_ge(sig["rstd2"], c + 1)
                    if due(16 * (h + u - 1)):
                        dve.wait_ge(n2_st[o], 16 * (h + u - 1))
                    v.tensor_scalar(n2[:, o, :], x2[:, o, :], mv2[:, 0:1], rs2[:, :], ALU.subtract,
                                    ALU.mult).then_inc(sig["n2_ready"], 1)
                rowmax(1)
                if has(b, 2):
                    if due(n + 1):
                        dve.wait_ge(sig["rstd1"], n + 1)
                    if due(n):
                        dve.wait_ge(sig["qrem"], n)
                    v.tensor_scalar(n1[:, :, :].rearrange("p (g k) d -> p k g d", g=G),
                                    xq[:, u, :].rearrange("p (k g d) -> p k g d", k=KV, g=G),
                                    mv1[:, 0:1], rs1[:, :], ALU.subtract, ALU.mult).then_inc(sig["n1_ready"], 1)
                rowmax(2)
                if has(b, 2):
                    if due(n + 1):
                        dve.wait_ge(sig["qcopy0"], n + 1)
                    if due(n):
                        dve.wait_ge(sig["qs_ready"], n)
                    v.tensor_tensor(rem[:, :, :], n1[:, :, :], qs[:, :, 0:DH], ALU.subtract).then_inc(sig["qrem"], 1)
                rowmax(3)
                if has(b, -1):
                    if due(c + 1):
                        dve.wait_ge(sig["lg"], c + 1)
                    v.tensor_reduce(nlm[:, :], ps[:, DB, 0:NEXP], X, ALU.max, negate=True).then_inc(sig["lgmax"], 1)
                rowmax(4)
                if has(b, 2):
                    if due(n + 1):
                        dve.wait_ge(sig["qcopy1"], n + 1)
                    v.tensor_tensor(qs[:, :, 5 * DH:6 * DH], rem[:, :, :], qs[:, :, 3 * DH:4 * DH],
                                    ALU.subtract).then_inc(sig["qs_ready"], 1)
                if has(b, -1):
                    if due(c + 1):
                        dve.wait_ge(sig["pexp"], c + 1)
                    v.reciprocal(rz[:, :], zs[:, :]).then_inc(sig["rz_ready"], 1)
                    if due(c + 1):
                        dve.wait_ge(sig["rz_ready"], c + 1)
                    v.tensor_scalar(sc[:, :], pe_[:, :], rz[:, :], None, ALU.mult).then_inc(sig["sc_ready"], 1)
                    if due(c + 1):
                        dve.wait_ge(sig["sc_ready"], c + 1)
                    settle(dve)
                    v.max(top[:, :], sc[:, :]).then_inc(sig["top_ready"], 1)
                    if due(c + 1):
                        dve.wait_ge(sig["top_ready"], c + 1)
                    settle(dve)
                    v.max_index(tix[:, :], top[:, :], sc[:, :]).then_inc(sig["tix_ready"], 1)
                    if due(c + 1):
                        dve.wait_ge(sig["tix_ready"], c + 1)
                    v.tensor_copy(ixf[:, :, 0], tix[:, 0:TOPK]).then_inc(sig["ixf_ready"], 1)
                    if due(c + 1):
                        dve.wait_ge(sig["ixf_ready"], c + 1)
                    v.tensor_tensor(oh[:, :, :], lane[:, :].unsqueeze(1).broadcast_to([P, TOPK, NEXP]),
                                    ixf[:, :, :].broadcast_to([P, TOPK, NEXP]), ALU.is_equal).then_inc(sig["oh_ready"], 1)
                    if due(c + 1):
                        dve.wait_ge(sig["oh_ready"], c + 1)
                    v.tensor_reduce(mk[:, :], oh[:, :, :].rearrange("p k e -> p e k"), X,
                                    ALU.add).then_inc(sig["mk_ready"], 1)
                    if due(c + 1):
                        dve.wait_ge(sig["mk_ready"], c + 1)
                    v.tensor_tensor(run[:, u, :], run[:, o, :], mk[:, :], ALU.add).then_inc(sig["run_ready"], 1)
                rowmax(5)
                if has(b, -1):
                    v.tensor_reduce(s6[:, :], top[:, 0:TOPK], X, ALU.add).then_inc(sig["s6_ready"], 1)
                    if due(c + 1):
                        dve.wait_ge(sig["s6_ready"], c + 1)
                    v.tensor_scalar(s6e[:, :], s6[:, :], 1e-20, None, ALU.add).then_inc(sig["s6e_ready"], 1)
                    if due(c + 1):
                        dve.wait_ge(sig["s6e_ready"], c + 1)
                    v.reciprocal(r6[:, :], s6e[:, :]).then_inc(sig["r6_ready"], 1)
                    if due(c + 1):
                        dve.wait_ge(sig["r6_ready"], c + 1)
                    if due(16 * TOPK * (h + u - 1)):
                        dve.wait_ge(pair_st[o], 16 * TOPK * (h + u - 1))
                    v.tensor_scalar(dat[:, o, :, 1], top[:, 0:TOPK], r6[:, :], None,
                                    ALU.mult).then_inc(sig["w_ready"], 1)
                    if due(2 * c):
                        dve.wait_ge(sig["tok_ready"], 2 * c)
                    v.tensor_copy(dat[:, o, :, 0], tok[:, :].broadcast_to([P, TOPK])).then_inc(sig["ids_ready"], 1)
                rowmax(6)
                if has(b, -1):
                    if due(c + 1):
                        dve.wait_ge(sig["pos"], c + 1)
                    v.tensor_tensor(pp[:, :, :], oh[:, :, :], ps[:, DB, 0:NEXP].unsqueeze(1).broadcast_to([P, TOPK, NEXP]),
                                    ALU.mult).then_inc(sig["pp_ready"], 1)
                    if due(c + 1):
                        dve.wait_ge(sig["pp_ready"], c + 1)
                    v.tensor_reduce(pk[:, :], pp[:, :, :], X, ALU.add).then_inc(sig["pk_ready"], 1)
                    if due(c + 1):
                        dve.wait_ge(sig["pk_ready"], c + 1)
                    v.tensor_scalar(va[:, :], pk[:, :], float(CAP), None, ALU.is_lt).then_inc(sig["va_ready"], 1)
                    v.scalar_tensor_tensor(sl0[:, :], ixf[:, :, 0], float(CAP), pk[:, :], ALU.mult,
                                           ALU.add).then_inc(sig["sl0_ready"], 1)
                    if due(c + 1):
                        dve.wait_ge(sig["sl0_ready"], c + 1)
                    v.tensor_tensor(sl1[:, :], sl0[:, :], trc[:, :], ALU.subtract).then_inc(sig["sl1_ready"], 1)
                    if due(c + 1):
                        dve.wait_ge(sig["sl1_ready"], c + 1)
                rowmax(7)
                if has(b, 1):
                    if due(KV * (b + 2)):
                        dve.wait_ge(sig["rowmax"], KV * (b + 2))
                    if due(b + 1):
                        dve.wait_ge(sig["m_tr"], b + 1)
                    mp = mm[:, :, :].rearrange("p g (i r) -> p g i r", i=2)
                    nv = nm[:, :, :].rearrange("p g (k i) -> p g i k", i=2)
                    v.tensor_copy(mp[:, :, :, 0:KV:2], nv).then_inc(sig["mm_hi"], 1)
                    if due(b + 2):
                        dve.wait_ge(sig["mm_hi"], b + 2)
                    v.tensor_tensor(mp[:, :, :, 1:KV:2], nv, mp[:, :, :, 0:KV:2],
                                    ALU.subtract).then_inc(sig["mm_ready"], 1)
                if has(b, -1):
                    if due(c + 1):
                        dve.wait_ge(sig["va_ready"], c + 1)
                    v.tensor_tensor(sl2[:, :], sl1[:, :], va[:, :], ALU.mult).then_inc(sig["sl2_ready"], 1)
                    if due(c + 1):
                        dve.wait_ge(sig["sl2_ready"], c + 1)
                    v.tensor_tensor(slot[:, o, :], sl2[:, :], trc[:, :], ALU.add).then_inc(sig["slot_ready"], 1)
                    if due(c + 1):
                        dve.wait_ge(sig["slot_ready"], c + 1)
                    if due(c + 1):
                        dve.wait_ge(sig["ids_ready"], c + 1)
                    v.tensor_scalar(tok[:, :], tok[:, :], float(P), None, ALU.add).then_inc(sig["tok_ready"], 1)
                    v.tensor_scalar(trc[:, :], trc[:, :], float(P), None, ALU.add).then_inc(sig["tok_ready"], 1)

            steps(dve, step)

            v.memset(hh[:, :, FF:D], 0.0).then_inc(sig["h_pad"], 1)

            for k in range(2):
                v.tensor_copy(ixg[:, k, :], idsT[:, 4 * k:4 * k + 4]).then_inc(sig["ixg_ready"], 1)

            def tile_list(i):
                if i == 1:
                    dve.wait_ge(sig["cnt"], 1)
                    v.tensor_scalar(cc[:, :], ps[:, LB, 0:NEXP], float(CAP), None, ALU.min).then_inc(sig["cc_ready"], 1)
                    dve.wait_ge(sig["cc_ready"], 1)
                    gt = oh[:, :, :].rearrange("p k e -> p (k e)").rearrange("p (e k) -> p e k", k=CAP_BLOCKS)
                    v.tensor_tensor(gt, cc[:, :].unsqueeze(2).broadcast_to([P, NEXP, CAP_BLOCKS]),
                                    thr[:, :].unsqueeze(1).broadcast_to([P, NEXP, CAP_BLOCKS]),
                                    ALU.is_gt).then_inc(sig["gt_ready"], 1)
                    dve.wait_ge(sig["gt_ready"], 1)
                    v.tensor_reduce(ntl[:, :], gt, X, ALU.add).then_inc(sig["nt_ready"], 1)
                    dve.wait_ge(sig["nt_ready"], 1)
                    v.tensor_tensor_scan(cum[:, :], ones[:, 0:NEXP], ntl[:, :], 0.0, ALU.mult,
                                         ALU.add).then_inc(sig["cum_ready"], 1)
                    dve.wait_ge(sig["cum_ready"], 1)
                    v.tensor_scalar(le[:, 0:NEXP - 1], cum[:, 0:NEXP - 1], jcol[:, :], None,
                                    ALU.is_le).then_inc(sig["le_ready"], 1)
                    dve.wait_ge(sig["le_ready"], 1)
                    v.tensor_reduce(ej[:, :], le[:, 0:NEXP - 1], X, ALU.add).then_inc(sig["ej_ready"], 1)
                if i == 2:
                    v.tensor_tensor(lec[:, 0:NEXP - 1], le[:, 0:NEXP - 1], cum[:, 0:NEXP - 1],
                                    ALU.mult).then_inc(sig["lec_ready"], 1)
                    dve.wait_ge(sig["lec_ready"], 1)
                    v.tensor_reduce(toj[:, :], lec[:, 0:NEXP - 1], X, ALU.max).then_inc(sig["toj_ready"], 1)
                    dve.wait_ge(sig["toj_ready"], 1)
                    v.tensor_tensor(jr[:, :], jcol[:, :], toj[:, :], ALU.subtract).then_inc(sig["jr_ready"], 1)
                    dve.wait_ge(sig["jr_ready"], 1)
                    dve.wait_ge(sig["ej_ready"], 1)
                    v.scalar_tensor_tensor(blk[:, :], ej[:, :], float(CAP_BLOCKS), jr[:, :], ALU.mult,
                                           ALU.add).then_inc(sig["blk_ready"], 1)
                if i == 3:
                    dve.wait_ge(sig["et_mm"], 1)
                    v.tensor_copy(etab[0:1, SH_TILES:TILES], ps[0:1, LB, 0:P]).then_inc(sig["et_ready"], 1)
                if i == 5:
                    dve.wait_ge(sig["idt_tr"], 1)
                    v.tensor_copy(idsT[:, SH_TILES:TILES], ps[:, LB, 0:P]).then_inc(sig["ids_all"], 1)
                    v.tensor_copy(wT[:, SH_TILES:TILES], ps[:, LB, P:2 * P]).then_inc(sig["wt_all"], 1)
                    dve.wait_ge(sig["ids_all"], 1)
                    dve.wait_ge(sig["wt_all"], 1)

            def x_copy(j, r):
                w = r % 2
                dve.wait_ge(sig["x_tr"], j + 1)
                if not isinstance(j, int) or j >= 2:
                    dve.wait_ge(sig["gu"], j - 1)
                v.tensor_copy(xT[:, w, :], ps[:, XB, 0:D]).then_inc(sig["xT_ready"], 1)

            def gated(j, r):
                w = r % 2
                dve.wait_ge(sig["sg_ready"], j + 1)
                if not isinstance(j, int) or j >= 2:
                    dve.wait_ge(sig["h_tr"], j - 1)
                v.tensor_tensor(hh[:, w, 0:FF], sg[:, w, :], ps[:, GB + w, FF:GU], ALU.mult).then_inc(sig["h_ready"], 1)

            def tile(j, m, r):
                if r % 4 == 0:
                    if not isinstance(j, int) or j >= 8:
                        for i in range(4):
                            dve.wait_ge(y_st[i], 32 * m + 16 * (r // 4) - 16)
                    v.tensor_copy(ixa[:, r // 4, :], idsT[:, bass.ds(j, 4)]).then_inc(sig["ixa_ready"], 1)
                    v.tensor_copy(wj[:, r // 4, :], wT[:, bass.ds(j, 4)]).then_inc(sig["ixa_ready"], 1)
                if not isinstance(j, int) or j + 1 < TILES:
                    gated(j + 1, r + 1)
                if isinstance(j, int):
                    tile_list(j)
                if not isinstance(j, int) or j + 2 < TILES:
                    x_copy(j + 2, r)
                if r % 4 == 3 and (not isinstance(j, int) or j + 5 < TILES):
                    dve.wait_ge(sig["x_tr"], j + 1)
                    v.tensor_copy(ixg[:, r // 4, :], idsT[:, bass.ds(j + 5, 4)]).then_inc(sig["ixg_ready"], 1)
            x_copy(0, 0)
            x_copy(1, 1)
            gated(0, 0)
            eights(dve, tile)

            for c in range(FCH):
                dve.wait_ge(f_in[c], 32)
                v.tensor_tensor(fa[:, c, :, :], fa[:, c, :, :], fb[:, c, :, :], ALU.add).then_inc(sig["fin_add"], 1)


def kernel(x, ctx_512, L0_ffn_wg_router, L0_ffn_w_gate, L0_ffn_w_up, L0_ffn_w_down,
           L0_ffn_ws_gate, L0_ffn_ws_up, L0_ffn_ws_down):
    import concourse.bacc as bacc
    from concourse.bass_utils import run_bass_kernel_spmd

    def rows(w):
        return w.reshape(w.shape[0], w.shape[1] // P, P, w.shape[2]).transpose(2, 0, 1, 3)

    a = [np.asarray(v) for v in (L0_ffn_w_gate, L0_ffn_w_up, L0_ffn_w_down, L0_ffn_ws_gate, L0_ffn_ws_up, L0_ffn_ws_down)]
    halves = lambda w: w.reshape(D, NSHARED, FF).transpose(1, 0, 2)
    gate = np.concatenate([a[0], halves(a[3])], axis=0)
    up = np.concatenate([a[1], halves(a[4])], axis=0)
    down = np.concatenate([a[2], a[5].reshape(NSHARED, FF, D)], axis=0)
    arrays = {
        "x": np.ascontiguousarray(x),
        "ctx": np.ascontiguousarray(ctx_512),
        "wrT": np.ascontiguousarray(np.asarray(L0_ffn_wg_router).T.reshape(2, P, NEXP).transpose(1, 0, 2)),
        "wgu": np.ascontiguousarray(np.concatenate([rows(gate), rows(up)], axis=3)),
        "wdn0": np.ascontiguousarray(down[:, :F0].transpose(1, 0, 2)),
        "wdn1": np.ascontiguousarray(down[:, F0:].transpose(1, 0, 2)),
    }
    nc = bacc.Bacc("TRN2", target_bir_lowering=False, num_devices=1)
    args = {n: nc.dram_tensor(n, v.shape, mybir.dt.from_np(v.dtype), kind="ExternalInput").ap() for n, v in arrays.items()}
    out = nc.dram_tensor("out", (B, S, D), F32, kind="ExternalOutput").ap()
    build(nc, out=out, **args)
    r = run_bass_kernel_spmd(nc, [arrays], core_ids=[0])
    return r.results[0]["out"]
```

```python
from contextlib import ExitStack

import numpy as np
import concourse.bass as bass
from concourse import mybir

F32 = mybir.dt.float32
BF16 = mybir.dt.bfloat16
U32 = mybir.dt.uint32
I32 = mybir.dt.int32
ALU = mybir.AluOpType
ACT = mybir.ActivationFunctionType
X = mybir.AxisListType.X

P = 128
B, S, D = 16, 128, 256
T = B * S
KV, G, DH = 8, 4, 8
HEADS = KV * G
NEXP, TOPK, FF = 32, 6, 176
CAP = 2 * (T * TOPK // NEXP)
CAP_BLOCKS = CAP // P
PARTS = 6
KROWS = PARTS * DH
KPAD = 64
VPAD = 32
KH = KV // 2
SCALE = float(1.0 / np.sqrt(np.float32(DH)))
LN_EPS = 1e-5
NSHARED = 2
NE2 = NEXP + NSHARED
SH_TILES = NSHARED * B
MOE_TILES = (T * TOPK) // P + NEXP
TILES = SH_TILES + MOE_TILES
BLOCKS = (NEXP - 1) * CAP_BLOCKS + MOE_TILES
ROWS = BLOCKS * P
TRASH = ROWS
PADROWS = T + P
GU = 2 * FF
F0, F1 = P, FF - P


def build(nc, x, ctx, wrT, wgu, wdn0, wdn1, out):
    n2_d = nc.dram_tensor("n2_rows", (PADROWS, D), F32, kind="Internal").ap()
    acc_d = [nc.dram_tensor(f"acc{i}", (PADROWS, D), F32, kind="Internal").ap() for i in range(2)]
    tab_d = nc.dram_tensor("pair_table", (ROWS + TOPK * T, 2), F32, kind="Internal").ap()
    es = ExitStack()
    with es:
        def sb(name, shape, dt=F32):
            return es.enter_context(nc.sbuf_tensor(name, shape, dt))

        def sem(name):
            return es.enter_context(nc.semaphore(name))

        wgu_s = sb("wgu_s", [P, NE2, 2, GU])
        wdn0_s = sb("wdn0_s", [P, NE2, D])
        wdn1_s = sb("wdn1_s", [F1, NE2, D])
        wr_s = sb("wr_s", [P, 2, NEXP])
        idf = sb("idf", [P, P])
        idb = sb("idb", [P, P], BF16)
        ones = sb("ones", [P, P])
        before = sb("before", [P, P])
        kvsel = sb("kvsel", [P, KV, P], BF16)
        lane = sb("lane", [P, NEXP])
        neghalf = sb("neghalf", [P, 1])
        jcol = sb("jcol", [P, 1])
        thr = sb("thr", [P, CAP_BLOCKS])
        xq = sb("xq", [P, 2, D])
        xr = sb("xr", [P, 2, D])
        cb = sb("cb", [P, 2, KV * DH])
        hT = sb("n1_rem_or_hT", [P, 2, D])
        n1, rem = [hT[:, i, :].rearrange("p (h d) -> p h d", d=DH) for i in range(2)]
        krem = sb("krem", [P, KV, DH])
        qs = sb("qs", [P, HEADS, KPAD], BF16)
        ks = sb("ks", [P, KV, KPAD], BF16)
        vx = sb("vx", [P, 2, KV, VPAD])
        OT = sb("OT", [P, G * S])
        arena = sb("qT_or_xg_yy", [P, 8, D])
        qT = arena[:, :, :].rearrange("p a d -> p (a d)").bitcast(BF16).rearrange(
            "p (u k s) -> p u k s", u=2, k=KV // 2)
        xg, yy = arena[:, 0:4, :], arena[:, 4:8, :]
        kT = sb("kT", [P, 2, KV // 2, S], BF16)
        nm = sb("nm", [P, G, KV])
        mm = sb("mm", [P, G, P], BF16)
        mT = sb("mT", [P, G * S], BF16)
        prx = sb("pr_or_xT_sg", [P, 2 * G * S])
        pr = prx[:, :].rearrange("p (u s) -> p u s", u=2)
        xT = prx[:, 0:2 * D].rearrange("p (u d) -> p u d", u=2)
        sg = prx[:, 2 * D:2 * D + 2 * FF].rearrange("p (u d) -> p u d", u=2)
        st1 = sb("st1", [P, 6])
        mv1 = sb("mv1", [P, 2])
        ve1 = sb("ve1", [P, 1])
        rs1 = sb("rs1", [P, 1])
        st2 = sb("st2", [P, 6])
        mv2 = sb("mv2", [P, 2])
        ve2 = sb("ve2", [P, 1])
        rs2 = sb("rs2", [P, 1])
        den = sb("den", [P, 2, KH, G, 1])
        hh = sb("at_n2T_or_h", [P, 2, D])
        at = hh[:, 0, :].rearrange("p (h d) -> p h d", d=DH)
        n2T = hh[:, 1, :].rearrange("p (c t) -> p c t", c=2)
        x2 = sb("x2", [P, 2, D])
        n2 = sb("n2", [P, 2, D])
        nlm = sb("nlm", [P, 1])
        pe_ = sb("pe_", [P, NEXP])
        zs = sb("zs", [P, 1])
        rz = sb("rz", [P, 1])
        sc = sb("sc", [P, NEXP])
        top = sb("top", [P, 8])
        tix = sb("tix", [P, 8], U32)
        s6 = sb("s6", [P, 1])
        s6e = sb("s6e", [P, 1])
        r6 = sb("r6", [P, 1])
        ixf = sb("ixf", [P, TOPK, 1])
        oh = sb("oh", [P, TOPK, NEXP])
        mk = sb("mk", [P, NEXP])
        run = sb("run", [P, 2, NEXP])
        pp = sb("pp", [P, TOPK, NEXP])
        pk = sb("pk", [P, TOPK])
        va = sb("va", [P, TOPK])
        sl0 = sb("sl0", [P, TOPK])
        sl1 = sb("sl1", [P, TOPK])
        sl2 = sb("sl2", [P, TOPK])
        tok = sb("tok", [P, 1])
        trc = sb("trc", [P, TOPK])
        slot = sb("slot", [P, 2, TOPK], U32)
        dat = sb("dat", [P, 2, TOPK, 2])
        idsT = sb("idsT", [P, TILES + 8])
        qsf = qs[:, :, :].rearrange("p h k -> p (h k)").bitcast(F32)
        wT = qsf[:, 0:TILES + 8]
        etab = qsf[0:1, TILES + 8:2 * (TILES + 8)].bitcast(I32)
        ixg = sb("ixg", [P, 2, 4], U32)
        ixa = sb("ixa", [P, 2, 4], U32)
        wj = sb("wj", [P, 2, 4])
        init = xg.rearrange("p a d -> p (a d)")[:, 0:2 * BLOCKS].rearrange(
            "p (r c) -> p r c", c=2)
        initi = yy.rearrange("p a d -> p (a d)")[:, 0:BLOCKS].bitcast(I32)
        zero = yy[:, 2, :]
        blk = sb("blk", [P, 1], U32)
        ej = sb("ej", [P, 1])
        toj = sb("toj", [P, 1])
        jr = sb("jr", [P, 1])
        cum, ntl, cc, le, lec = [OT[:, i * NEXP:(i + 1) * NEXP] for i in range(5)]
        g2 = x2[:, 0, :].rearrange("p (r c) -> p r c", c=2)
        FCH = 4
        wflat = wgu_s[:, :, :, :].rearrange("p e c f -> p (e c f)")
        fa, fb = [wflat[:, i * B * D:(i + 1) * B * D].rearrange("p (c a d) -> p c a d", c=FCH, d=D)
                  for i in range(2)]

        ps = es.enter_context(nc.psum_tensor("ps", [P, 8, 512], F32))
        psb = ps[:, :, :].bitcast(BF16)
        SM, SE, CQ, OB, DB = 0, 2, 4, 5, 7
        XB, LB, GB, HB, YB = 0, 1, 2, 4, 6

        names = """held const_pool const_dve init_iota init_and init_add init_zero init_done wr_in w_in
        kc0 kc1 kc2 kc3 ks_ready vx_ready stat1 mean1 veps1 rstd1 n1_ready qcopy0 qrem qcopy1 qs_ready
        q_tr k_tr m_tr q_ev k_ev m_ev s1 s2 pv rowmax mm_hi mm_ready expd
        o_ev o_tr den_ready o_free x2_ready stat2 mean2 veps2 rstd2 n2_ready n2_tr n2_ev lg lgmax pexp
        rz_ready sc_ready top_ready tix_ready s6_ready s6e_ready r6_ready w_ready ixf_ready
        oh_ready mk_ready run_ready pos pp_ready pk_ready va_ready sl0_ready sl1_ready sl2_ready slot_ready ids_ready
        tok_ready trc_ready own_init w_init cnt cc_ready gt_ready nt_ready cum_ready le_ready ej_ready lec_ready toj_ready jr_ready
        blk_ready h_pad g2_in et_mm et_ready idt_tr ids_all wt_all
        ixg_ready ixa_ready x_tr xT_ready gu sg_ready h_ready h_tr hT_ready dn y_ready
        fin_add fin_done""".split()
        sig = {n: sem(n) for n in names}
        xq_in = [sem(f"xq_in{i}") for i in range(2)]
        xr_in = [sem(f"xr_in{i}") for i in range(2)]
        c_in = [sem(f"c_in{i}") for i in range(2)]
        x2_st = [sem(f"x2_st{i}") for i in range(2)]
        n2_st = [sem(f"n2_st{i}") for i in range(2)]
        pair_st = [sem(f"pair_st{i}") for i in range(2)]
        g_in = [sem(f"g_in{i}") for i in range(4)]
        y_st = [sem(f"y_st{i}") for i in range(4)]
        f_in = [sem(f"f_in{i}") for i in range(FCH)]
        f_st = sem("f_st")
        NCONST_POOL = 14

        block = es.enter_context(nc.Block())

        def due(n):
            return not isinstance(n, int) or n > 0

        def settle(eng):
            eng.sem_inc(sig["held"], 1)

        def steps(eng, step):
            for b in (-2, -1, 0, 1):
                step(b, b // 2, b % 2)
            with eng.Fori(1, B // 2 - 1) as h:
                for u in range(2):
                    step(2 * h + u, h, u)
            for b in range(B - 2, B + 2):
                step(b, b // 2, b % 2)

        def has(b, off):
            return not isinstance(b, int) or 0 <= b + off < B

        AHEAD = 4

        def eights(eng, tile):
            for r in range(8):
                tile(r, 0, r)
            with eng.Fori(1, TILES // 8 - 1) as m:
                for r in range(8):
                    tile(8 * m + r, m, r)
            for r in range(8):
                tile(TILES - 8 + r, TILES // 8 - 1, r)

        @block.sync
        def _(sp):
            def load_q(b, h, u):
                sp.dma_start(xq[:, u, :], x[bass.ds(b, 1), :, :].rearrange("a p d -> p (a d)")).then_inc(xq_in[u], 16)
                sp.dma_start(cb[:, u, :], ctx[bass.ds(b, 1), :, :].rearrange("a p d -> p (a d)")).then_inc(c_in[u], 16)

            def load_r(b, u):
                sp.dma_start(xr[:, u, :], x[bass.ds(b, 1), :, :].rearrange("a p d -> p (a d)")).then_inc(xr_in[u], 16)

            load_q(0, 0, 0)
            sp.dma_start(wr_s[:, :, :], wrT).then_inc(sig["wr_in"], 16)
            sp.wait_ge(sig["init_zero"], 1)
            for i in range(B + 1):
                sp.dma_start(acc_d[1][i * P:(i + 1) * P, :], zero).then_inc(sig["init_done"], 16)
            sp.dma_start(acc_d[0][T:PADROWS, :], zero).then_inc(sig["init_done"], 16)
            sp.dma_start(n2_d[T:PADROWS, :], zero).then_inc(sig["init_done"], 16)
            sp.wait_ge(sig["init_add"], 2)
            sp.dma_start(tab_d[0:ROWS, :].rearrange("(p r) c -> p r c", p=P), init).then_inc(sig["init_done"], 16)

            def step(b, h, u):
                o = 1 - u
                if has(b, -1):
                    if due(b):
                        sp.wait_ge(sig["x2_ready"], b)
                    sp.dma_start(acc_d[0][bass.ds((b - 1) * P, P), :], x2[:, o, :]).then_inc(x2_st[o], 16)
                if has(b, 1):
                    load_r(b + 1, o)
                if has(b, -1):
                    if due(b):
                        sp.wait_ge(sig["n2_ready"], b)
                    sp.dma_start(n2_d[bass.ds((b - 1) * P, P), :], n2[:, o, :]).then_inc(n2_st[o], 16)
                if has(b, 0):
                    e = 2 * b
                    sp.dma_start(wgu_s[:, bass.ds(e, 2), :, :], wgu[:, bass.ds(e, 2), :, :]).then_inc(sig["w_in"], 16)
                    sp.dma_start(wdn0_s[:, bass.ds(e, 2), :], wdn0[:, bass.ds(e, 2), :]).then_inc(sig["w_in"], 16)
                    sp.dma_start(wdn1_s[:, bass.ds(e, 2), :], wdn1[:, bass.ds(e, 2), :]).then_inc(sig["w_in"], 16)
                if has(b, 3):
                    if due(b + 2):
                        sp.wait_ge(sig["n1_ready"], b + 2)
                        sp.wait_ge(sig["vx_ready"], b + 2)
                    load_q(b + 3, h, o)

            for b in (-2, -1, 0, 1):
                step(b, b // 2, b % 2)
            with sp.Fori(1, B // 2 - 2) as h:
                for u in range(2):
                    step(2 * h + u, h, u)
            for b in range(B - 4, B + 2):
                step(b, b // 2, b % 2)
            e = NEXP
            sp.dma_start(wgu_s[:, e:, :, :], wgu[:, e:, :, :]).then_inc(sig["w_in"], 16)
            sp.dma_start(wdn0_s[:, e:, :], wdn0[:, e:, :]).then_inc(sig["w_in"], 16)
            sp.dma_start(wdn1_s[:, e:, :], wdn1[:, e:, :]).then_inc(sig["w_in"], 16)

            for i in range(4):
                sp.wait_ge(y_st[i], 16 * (TILES // 4))
            fv = [a[0:T, :].rearrange("(c a p) d -> c p a d", p=P, c=FCH) for a in acc_d]
            ov = out.rearrange("(c a) p d -> c p a d", c=FCH)
            for c in range(FCH):
                sp.dma_start(fa[:, c, :, :], fv[0][c]).then_inc(f_in[c], 16)
                sp.dma_start(fb[:, c, :, :], fv[1][c]).then_inc(f_in[c], 16)
            for c in range(FCH):
                sp.wait_ge(sig["fin_add"], c + 1)
                sp.dma_start(ov[c], fa[:, c, :, :]).then_inc(f_st, 16)
            sp.wait_ge(f_st, 16 * FCH)

        @block.gpsimd
        def _(pool):
            g = nc.gpsimd
            cp = sig["const_pool"]
            g.memset(idf[:, :], 0.0).then_inc(cp, 1)
            g.memset(idb[:, :], 0.0).then_inc(cp, 1)
            g.memset(before[:, :], 1.0).then_inc(cp, 1)
            g.memset(kvsel[:, :, :], 1.0).then_inc(cp, 1)
            g.memset(vx[:, :, :, :], 0.0).then_inc(cp, 1)
            g.iota(initi, [[1, BLOCKS]], base=0, channel_multiplier=BLOCKS % P).then_inc(sig["init_iota"], 1)
            pool.wait_ge(cp, 5)
            for m in (idf, idb):
                g.affine_select(out=m[:, :], in_=m[:, :], compare_op=ALU.not_equal, fill=1.0, base=0,
                                pattern=[[-1, P]], channel_multiplier=1).then_inc(cp, 1)
            g.affine_select(out=before[:, :], in_=before[:, :], compare_op=ALU.is_gt, fill=0.0, base=0,
                            pattern=[[1, P]], channel_multiplier=-1).then_inc(cp, 1)
            ksv = kvsel[:, :, :].rearrange("p (a b) c -> p a b c", b=2)
            g.affine_select(out=ksv, in_=ksv, compare_op=ALU.is_ge, fill=0.0, base=0,
                            pattern=[[-2, KV // 2], [-KPAD, 2], [0, P]], channel_multiplier=1).then_inc(cp, 1)
            pool.wait_ge(cp, 9)
            g.affine_select(out=ksv, in_=ksv, compare_op=ALU.is_ge, fill=0.0, base=1,
                            pattern=[[2, KV // 2], [KPAD, 2], [0, P]], channel_multiplier=-1).then_inc(cp, 1)
            g.iota(lane[:, :], [[1, NEXP]], base=0, channel_multiplier=0, allow_small_or_imprecise_dtypes=True)
            g.iota(jcol[:, :], [[1, 1]], base=0, channel_multiplier=1, allow_small_or_imprecise_dtypes=True)
            g.iota(thr[:, :], [[P, CAP_BLOCKS]], base=0, channel_multiplier=0, allow_small_or_imprecise_dtypes=True)
            g.iota(tok[:, :], [[1, 1]], base=0, channel_multiplier=1, allow_small_or_imprecise_dtypes=True)
            g.iota(trc[:, :], [[T, TOPK]], base=TRASH, channel_multiplier=1, allow_small_or_imprecise_dtypes=True)
            g.iota(idsT[:, 0:SH_TILES], [[P, B], [0, NSHARED]], base=0, channel_multiplier=1,
                   allow_small_or_imprecise_dtypes=True)
            g.memset(neghalf[:, :], -0.5)
            g.memset(vx[:, :, :, DH:DH + 1], 1.0).then_inc(cp, 4)

            def rstd(var, veps, dst, s0, s1, b):
                settle(pool)
                g.tensor_scalar(veps[:, :], var, LN_EPS, None, ALU.add).then_inc(s0, 1)
                if due(b + 1):
                    pool.wait_ge(s0, b + 1)
                g.tensor_tensor(dst[:, :], veps[:, :], neghalf[:, :], ALU.pow).then_inc(s1, 1)

            def step(b, h, u):
                o = 1 - u
                if has(b, 2):
                    n = b + 2
                    pool.wait_ge(sig["mean1"], n + 1)
                    if due(n):
                        pool.wait_ge(sig["n1_ready"], n)
                    rstd(mv1[:, 1:2], ve1, rs1, sig["veps1"], sig["rstd1"], n)
                if has(b, 1):
                    if due(KV * b):
                        pool.wait_ge(sig["pv"], KV * b)
                    if isinstance(b, int) and b == -1:
                        pool.wait_ge(c_in[o], 16)
                    settle(pool)
                    g.tensor_copy(vx[:, o, :, 0:DH], cb[:, o, :].rearrange("p (k d) -> p k d", d=DH)
                                  ).then_inc(sig["vx_ready"], 1)
                if has(b, -1):
                    pool.wait_ge(sig["mean2"], b)
                    rstd(mv2[:, 1:2], ve2, rs2, sig["veps2"], sig["rstd2"], b - 1)
                if has(b, 2):
                    pool.wait_ge(c_in[u], 16 * (h + 2))
                    if due(n):
                        pool.wait_ge(sig["k_tr"], n)
                    c3 = cb[:, u, :].rearrange("p (k d) -> p k d", d=DH)
                    kv4 = ks[:, :, 0:KROWS].rearrange("p k (j d) -> p k j d", d=DH)
                    kj = [kv4[:, :, j, :] for j in range(PARTS)]
                    settle(pool)
                    g.tensor_copy(kj[0], c3).then_inc(sig["kc0"], 1)
                    g.tensor_copy(kj[3], c3)
                    g.tensor_copy(kj[5], c3)
                    pool.wait_ge(sig["kc0"], n + 1)
                    g.tensor_tensor(krem[:, :, :], c3, kj[0], ALU.subtract).then_inc(sig["kc1"], 1)
                    pool.wait_ge(sig["kc1"], n + 1)
                    settle(pool)
                    g.tensor_copy(kj[1], krem[:, :, :]).then_inc(sig["kc2"], 1)
                    g.tensor_copy(kj[4], krem[:, :, :])
                    pool.wait_ge(sig["kc2"], n + 1)
                    g.tensor_tensor(kj[2], krem[:, :, :], kj[1], ALU.subtract).then_inc(sig["ks_ready"], 1)
                if has(b, -2):
                    pool.wait_ge(sig["slot_ready"], b - 1)
                    pool.wait_ge(sig["ids_ready"], b - 1)
                    settle(pool)
                    for k in range(TOPK):
                        g.indirect_dma_start(tab_d, bass.IndirectOffsetOnAxis(ap=slot[:, u, k:k + 1], axis=0),
                                             dat[:, u, k, :], None).then_inc(pair_st[u], 16)

            steps(pool, step)

            def gather(j, m, r):
                if r % 4 == 0:
                    pool.wait_ge(sig["ixg_ready"], 2 * m + r // 4 + 1)
                if not isinstance(j, int) or j >= 4:
                    pool.wait_ge(sig["x_tr"], j - 3)
                settle(pool)
                g.indirect_dma_start(xg[:, r % 4, :], None, n2_d,
                                     bass.IndirectOffsetOnAxis(ap=ixg[:, r // 4, r % 4:r % 4 + 1], axis=0)
                                     ).then_inc(g_in[r % 4], 16)

            def add(j, m, r):
                pool.wait_ge(sig["y_ready"], j + 1)
                if r % 4 == 0:
                    pool.wait_ge(sig["ixa_ready"], 4 * m + 2 * (r // 4) + 2)
                if r >= 2:
                    pool.wait_ge(y_st[(r - 2) % 4], 32 * m + 16 * ((r - 2) // 4 + 1))
                elif not isinstance(m, int) or m > 0:
                    pool.wait_ge(y_st[r + 2], 32 * m)
                settle(pool)
                g.indirect_dma_start(acc_d[r % 2], bass.IndirectOffsetOnAxis(ap=ixa[:, r // 4, r % 4:r % 4 + 1], axis=0),
                                     yy[:, r % 4, :], None, compute_op=ALU.add).then_inc(y_st[r % 4], 16)

            g.iota(etab[0:1, 0:SH_TILES], [[0, B], [1, NSHARED]], base=NEXP, channel_multiplier=0).then_inc(sig["own_init"], 1)
            for i in range(2):
                pool.wait_ge(n2_st[i], 16 * (B // 2))
                pool.wait_ge(x2_st[i], 16 * (B // 2))
            for j in range(AHEAD):
                gather(j, 0, j)
            pool.wait_ge(sig["blk_ready"], 1)
            for i in range(2):
                pool.wait_ge(pair_st[i], 16 * TOPK * (B // 2))
            g.indirect_dma_start(x2[:, 0, :], None, tab_d[0:ROWS, :].rearrange("(b r) c -> b (r c)", r=P),
                                 bass.IndirectOffsetOnAxis(ap=blk[:, :], axis=0)).then_inc(sig["g2_in"], 16)

            def tile(j, m, r):
                if not isinstance(j, int) or j + AHEAD < TILES:
                    gather(j + AHEAD, m + (r + AHEAD) // 8, (r + AHEAD) % 8)
                add(j, m, r)
            eights(pool, tile)

        @block.scalar
        def _(act):
            a = nc.scalar

            def step(b, h, u):
                o = 1 - u
                if has(b, 0):
                    act.wait_ge(sig["m_tr"], b + 1)
                    if due(KV * b):
                        act.wait_ge(sig["s2"], KV * b)
                    a.activation(mT[:, :], psb[:, DB, 0:G * S], ACT.Copy).then_inc(sig["m_ev"], 1)
                if has(b, -1):
                    act.wait_ge(sig["pv"], KV * b)
                    act.wait_ge(sig["o_tr"], 2 * b - 1)
                    a.activation(OT[:, :], ps[:, OB + 1, :], ACT.Copy).then_inc(sig["o_ev"], 1)
                for kv in range(KV):
                    if has(b, 0):
                        n = KV * b + kv
                        act.wait_ge(sig["s2"], n + 1)
                        if due(n - 1):
                            act.wait_ge(sig["pv"], n - 1)
                        a.activation(pr[:, kv % 2, :], ps[:, SE + kv % 2, :], ACT.Exp,
                                     scale=SCALE).then_inc(sig["expd"], 1)
                    if kv == 0 and has(b, 1):
                        act.wait_ge(sig["q_tr"], 2 * (b + 1) + 2)
                        a.activation(qT[:, o, 2:4, :], psb[:, CQ, :], ACT.Copy).then_inc(sig["q_ev"], 1)
                    if kv == 2 and has(b, 2):
                        act.wait_ge(sig["n1_ready"], b + 3)
                        a.activation(qs[:, :, 0:3 * DH].rearrange("p h (j d) -> p h j d", d=DH),
                                     n1.unsqueeze(2).broadcast_to([P, HEADS, 3, DH]),
                                     ACT.Copy).then_inc(sig["qcopy0"], 1)
                    if kv == 3 and has(b, -1):
                        act.wait_ge(sig["n2_tr"], b)
                        if due(b - 1):
                            act.wait_ge(sig["lg"], b - 1)
                        a.activation(n2T[:, :, :], ps[:, DB, 0:D], ACT.Copy).then_inc(sig["n2_ev"], 1)
                    if kv == 4 and has(b, 2):
                        act.wait_ge(sig["qrem"], b + 3)
                        a.activation(qs[:, :, 3 * DH:5 * DH].rearrange("p h (j d) -> p h j d", d=DH),
                                     rem.unsqueeze(2).broadcast_to([P, HEADS, 2, DH]),
                                     ACT.Copy).then_inc(sig["qcopy1"], 1)
                    if kv == 5 and has(b, 0):
                        act.wait_ge(sig["pv"], KV * b + KH)
                        if due(2 * b):
                            act.wait_ge(sig["o_tr"], 2 * b)
                        a.activation(OT[:, :], ps[:, OB, :], ACT.Copy).then_inc(sig["o_ev"], 1)
                    if kv == 5 and has(b, -1):
                        act.wait_ge(sig["lgmax"], b)
                        a.activation(pe_[:, :], ps[:, DB, 0:NEXP], ACT.Exp, bias=nlm[:, :],
                                     accum_out=zs[:, :]).then_inc(sig["pexp"], 1)
                    if kv == 6 and has(b, 2):
                        act.wait_ge(sig["q_tr"], 2 * (b + 2) + 1)
                        if isinstance(b, int) and b == -2:
                            act.wait_ge(sig["init_done"], 16 * (B + 4))
                        a.activation(qT[:, u, 0:2, :], psb[:, CQ, :], ACT.Copy).then_inc(sig["q_ev"], 1)
                if has(b, 2):
                    act.wait_ge(sig["k_tr"], b + 3)
                    a.activation(kT[:, u, :, :], psb[:, DB, 0:KV // 2 * S], ACT.Copy).then_inc(sig["k_ev"], 1)

            steps(act, step)

            def scaled(j, m, r):
                act.wait_ge(sig["dn"], j + 1)
                if r % 4 == 0:
                    act.wait_ge(sig["ixa_ready"], 4 * m + 2 * (r // 4) + 2)
                if not isinstance(j, int) or j >= 4:
                    act.wait_ge(y_st[r % 4], 32 * m + 16 * (r // 4))
                a.activation(yy[:, r % 4, :], ps[:, YB + r % 2, 0:D], ACT.Copy,
                             scale=wj[:, r // 4, r % 4:r % 4 + 1]).then_inc(sig["y_ready"], 1)

            def silu(j, r):
                w = r % 2
                act.wait_ge(sig["gu"], j + 1)
                if not isinstance(j, int) or j >= 2:
                    act.wait_ge(sig["h_ready"], j - 1)
                a.activation(sg[:, w, :], ps[:, GB + w, 0:FF], ACT.Silu).then_inc(sig["sg_ready"], 1)

            def tile(j, m, r):
                w = r % 2
                act.wait_ge(sig["h_tr"], j + 1)
                if not isinstance(j, int) or j >= 2:
                    act.wait_ge(sig["dn"], j - 1)
                a.activation(hT[:, w, :], ps[:, HB + w, 0:D], ACT.Copy).then_inc(sig["hT_ready"], 1)
                if not isinstance(j, int) or j + 1 < TILES:
                    silu(j + 1, r + 1)
                scaled(j, m, r)
            silu(0, 0)
            eights(act, tile)

        @block.tensor
        def _(pe):
            t = nc.tensor
            pe.wait_ge(sig["const_pool"], NCONST_POOL)
            pe.wait_ge(sig["const_dve"], 1)

            def q_transposes(b, half):
                for pr_ in range(2):
                    for g in range(G):
                        pair = 2 * half + pr_
                        h0 = g * KV + 2 * pair
                        last = t.transpose(psb[:, CQ, (pr_ * G + g) * S:(pr_ * G + g + 1) * S],
                                           qs[:, h0:h0 + 2, :].rearrange("p h k -> p (h k)"), idb[:, :])
                last.then_inc(sig["q_tr"], 1)

            def o_transposes(half):
                for g in range(G):
                    last = t.transpose(ps[:, OB + half, g * S:(g + 1) * S], OT[:, g * S:(g + 1) * S], idf[:, :])
                last.then_inc(sig["o_tr"], 1)

            def step(b, h, u):
                o = 1 - u
                if has(b, -1):
                    pv(b - 1, KV - 1, o)
                if has(b, 0):
                    pe.wait_ge(sig["mm_ready"], b + 1)
                    if has(b, 1):
                        pe.wait_ge(sig["k_ev"], b + 2)
                    else:
                        pe.wait_ge(sig["pexp"], b - 1)
                    for g in range(G):
                        last = t.transpose(psb[:, DB, g * S:(g + 1) * S], mm[:, g, :], idb[:, :])
                    last.then_inc(sig["m_tr"], 1)
                if has(b, 1):
                    pe.wait_ge(sig["q_ev"], 2 * (b + 1) + 1)
                    q_transposes(b + 1, 1)
                for kv in range(KV):
                    p0, pair = KPAD * (kv % 2), kv // 2
                    if has(b, 1):
                        n = KV * (b + 1) + kv
                        if due(n - 1):
                            pe.wait_ge(sig["rowmax"], n - 1)
                        if kv == 0 and not has(b, 0):
                            pe.wait_ge(sig["k_ev"], b + 2)
                        if kv == KH:
                            pe.wait_ge(sig["q_ev"], 2 * (b + 1) + 2)
                        for g in range(G):
                            last = t.matmul(ps[:, SM + kv % 2, g * S:(g + 1) * S],
                                            qT[p0:p0 + KROWS, o, pair, g * S:(g + 1) * S],
                                            kT[p0:p0 + KROWS, o, pair, :], start=True, stop=True)
                        last.then_inc(sig["s1"], 1)
                    if has(b, 0):
                        n = KV * b + kv
                        if due(n - 1):
                            pe.wait_ge(sig["expd"], n - 1)
                        if kv == 0:
                            pe.wait_ge(sig["m_ev"], b + 1)
                        t.matmul(ps[:, SE + kv % 2, :], kT[p0:p0 + KROWS, u, pair, :], qT[p0:p0 + KROWS, u, pair, :],
                                 start=True, stop=False)
                        t.matmul(ps[:, SE + kv % 2, :], kvsel[p0:p0 + KPAD, kv, :], mT[p0:p0 + KPAD, :],
                                 start=False, stop=True).then_inc(sig["s2"], 1)
                    if kv == 1 and has(b, -2):
                        pe.wait_ge(sig["run_ready"], b - 1)
                        if not has(b, 0):
                            pe.wait_ge(sig["pexp"], b - 1)
                        t.matmul(ps[:, DB, 0:NEXP], before[:, :], mk[:, :], start=True, stop=False)
                        t.matmul(ps[:, DB, 0:NEXP], ones[:, :], run[:, u, :],
                                 start=False, stop=True).then_inc(sig["pos"], 1)
                    if kv == 1 and has(b, -1):
                        pe.wait_ge(sig["o_ev"], 2 * b)
                        o_transposes(1)
                    if kv >= 1 and has(b, 0):
                        pv(b, kv - 1, u)
                    if kv == 3 and has(b, -1):
                        pe.wait_ge(sig["n2_ready"], b)
                        if due(b - 1):
                            pe.wait_ge(sig["pp_ready"], b - 1)
                        for c in range(2):
                            last = t.transpose(ps[:, DB, c * P:(c + 1) * P], n2[:, o, c * P:(c + 1) * P], idf[:, :])
                        last.then_inc(sig["n2_tr"], 1)
                    if kv == 4 and has(b, -1):
                        pe.wait_ge(sig["n2_ev"], b)
                        if isinstance(b, int) and b == 1:
                            pe.wait_ge(sig["wr_in"], 16)
                        for c in range(2):
                            last = t.matmul(ps[:, DB, 0:NEXP], n2T[:, c, :], wr_s[:, c, :],
                                            start=(c == 0), stop=(c == 1))
                        last.then_inc(sig["lg"], 1)
                    if kv == 6 and has(b, 0):
                        pe.wait_ge(sig["o_ev"], 2 * b + 1)
                        o_transposes(0)
                    if kv == 6 and has(b, 2):
                        pe.wait_ge(sig["qs_ready"], b + 3)
                        if due(2 * (b + 2)):
                            pe.wait_ge(sig["q_ev"], 2 * (b + 2))
                        q_transposes(b + 2, 0)
                    if kv == 7 and has(b, 2):
                        pe.wait_ge(sig["ks_ready"], b + 3)
                        if due(b):
                            pe.wait_ge(sig["pexp"], b)
                        elif isinstance(b, int) and b == -1:
                            pe.wait_ge(sig["k_ev"], b + 2)
                        for pair in range(KV // 2):
                            last = t.transpose(psb[:, DB, pair * S:(pair + 1) * S],
                                               ks[:, 2 * pair:2 * pair + 2, :].rearrange("p h k -> p (h k)"), idb[:, :])
                        last.then_inc(sig["k_tr"], 1)

            def pv(b, kv, u):
                half, p0 = kv // KH, VPAD * (kv % KH)
                pe.wait_ge(sig["expd"], KV * b + kv + 1)
                if kv % KH == 0:
                    if due(2 * b + half - 1):
                        pe.wait_ge(sig["o_free"], 2 * b + half - 1)
                    if kv == 0:
                        pe.wait_ge(sig["vx_ready"], b + 1)
                t.matmul(ps[p0:p0 + VPAD, OB + half, :], vx[:, u, kv, :], pr[:, kv % 2, :],
                         start=True, stop=True).then_inc(sig["pv"], 1)

            steps(pe, step)

            def tile_list(i):
                if i == 0:
                    t.matmul(ps[:, LB, 0:NEXP], ones[:, :], run[:, 0, :], start=True, stop=True).then_inc(sig["cnt"], 1)
                if i == 2:
                    pe.wait_ge(sig["ej_ready"], 1)
                    t.matmul(ps[0:1, LB, 0:P], ej[:, :], idf[:, :], start=True, stop=True).then_inc(sig["et_mm"], 1)
                if i == 4:
                    pe.wait_ge(sig["et_ready"], 1)
                    pe.wait_ge(sig["g2_in"], 16)
                    for c in range(2):
                        last = t.transpose(ps[:, LB, c * P:(c + 1) * P], g2[:, :, c], idf[:, :])
                    last.then_inc(sig["idt_tr"], 1)

            def x_transpose(j, m, r):
                pe.wait_ge(g_in[r % 4], 32 * m + 16 * (r // 4 + 1))
                for c in range(2):
                    last = t.transpose(ps[:, XB, c * P:(c + 1) * P], xg[:, r % 4, c * P:(c + 1) * P], idf[:, :])
                last.then_inc(sig["x_tr"], 1)

            def expert_of(j):
                return nc.values_load(etab[0:1, bass.ds(j, 1)], engines=(mybir.EngineType.PE,), min_val=0, max_val=NE2 - 1,
                                      skip_runtime_bounds_check_because="a sum of 31 comparisons, or one of the shared halves")

            def gate_up(j, r, e):
                w = r % 2
                pe.wait_ge(sig["xT_ready"], j + 1)
                for c in range(2):
                    last = t.matmul(ps[:, GB + w, 0:GU], xT[:, w, c * P:(c + 1) * P],
                                    wgu_s[:, bass.ds(e, 1), c, :].rearrange("p a f -> p (a f)"),
                                    start=(c == 0), stop=(c == 1))
                last.then_inc(sig["gu"], 1)

            def h_transpose(j, r):
                w = r % 2
                pe.wait_ge(sig["h_ready"], j + 1)
                for c in range(2):
                    last = t.transpose(ps[:, HB + w, c * P:(c + 1) * P], hh[:, w, c * P:(c + 1) * P], idf[:, :])
                last.then_inc(sig["h_tr"], 1)

            def down(j, r, e):
                w = r % 2
                pe.wait_ge(sig["hT_ready"], j + 1)
                t.matmul(ps[:, YB + w, 0:D], hT[:, w, 0:P],
                         wdn0_s[:, bass.ds(e, 1), :].rearrange("p a f -> p (a f)"), start=True, stop=False)
                t.matmul(ps[:, YB + w, 0:D], hT[0:F1, w, P:2 * P],
                         wdn1_s[:, bass.ds(e, 1), :].rearrange("p a f -> p (a f)"),
                         start=False, stop=True).then_inc(sig["dn"], 1)

            pe.wait_ge(sig["w_in"], 16 * 3 * (NE2 // 2))
            x_transpose(0, 0, 0)
            pe.wait_ge(sig["xT_ready"], 1)
            x_transpose(1, 0, 1)
            gate_up(0, 0, NEXP)
            pe.wait_ge(sig["run_ready"], B)
            pe.wait_ge(sig["pp_ready"], B)
            pe.wait_ge(sig["h_pad"], 1)
            pe.wait_ge(sig["own_init"], 1)

            expert = {}

            def tile(j, m, r):
                if isinstance(j, int):
                    tile_list(j)
                if r == 0:
                    expert[0] = expert_of(j)
                last_one = isinstance(j, int) and j + 1 == TILES
                if not last_one:
                    expert[1] = expert_of(j + 1)
                h_transpose(j, r)
                if not last_one:
                    gate_up(j + 1, r + 1, expert[1])
                if not isinstance(j, int) or j + 2 < TILES:
                    x_transpose(j + 2, m + (r + 2) // 8, (r + 2) % 8)
                down(j, r, expert[0])
                expert[0] = expert[1]
            eights(pe, tile)

        @block.vector
        def _(dve):
            v = nc.vector
            v.memset(zero, 0.0).then_inc(sig["init_zero"], 1)
            v.memset(ones[:, :], 1.0)
            v.memset(qs[:, :, :], 0.0)
            v.memset(ks[:, :, :], 0.0)
            v.memset(mm[:, :, :], 0.0)
            v.memset(run[:, 0, :], 0.0).then_inc(sig["const_dve"], 1)
            v.memset(init[:, :, 1:2], 0.0).then_inc(sig["init_add"], 1)
            dve.wait_ge(sig["init_iota"], 1)
            v.tensor_scalar(initi, initi, P - 1, None, ALU.bitwise_and).then_inc(sig["init_and"], 1)
            dve.wait_ge(sig["init_and"], 1)
            v.tensor_scalar(init[:, :, 0:1].rearrange("p r c -> p (r c)"), initi, float(T), None,
                            ALU.add).then_inc(sig["init_add"], 1)
            dve.wait_ge(sig["const_pool"], NCONST_POOL)

            def step(b, h, u):
                o = 1 - u

                def rowmax(kv):
                    if has(b, 1):
                        n = KV * (b + 1) + kv
                        if due(n + 1):
                            dve.wait_ge(sig["s1"], n + 1)
                        if kv == 0:
                            if due(b + 1):
                                dve.wait_ge(sig["mm_ready"], b + 1)
                        v.tensor_reduce(nm[:, :, kv], ps[:, SM + kv % 2, :].rearrange("p (g t) -> p g t", g=G),
                                        X, ALU.max, negate=True).then_inc(sig["rowmax"], 1)

                def result(c, half):
                    dve.wait_ge(sig["o_tr"], 2 * c + half + 1)
                    O = ps[:, OB + half, :].rearrange("p (g k d) -> p k g d", g=G, k=KH)
                    v.reciprocal(den[:, half, :, :, :], O[:, :, :, DH:DH + 1]).then_inc(sig["den_ready"], 1)
                    dve.wait_ge(sig["den_ready"], 2 * c + half + 1)
                    v.tensor_tensor(at[:, half * HEADS // 2:(half + 1) * HEADS // 2, :].rearrange("p (k g) d -> p k g d", g=G),
                                    O[:, :, :, 0:DH], den[:, half, :, :, :].broadcast_to([P, KH, G, DH]),
                                    ALU.mult).then_inc(sig["o_free"], 1)

                rowmax(0)
                if has(b, 2):
                    n = b + 2
                    dve.wait_ge(xq_in[u], 16 * (h + 2))
                    v.bn_stats(st1[:, :], xq[:, u, :]).then_inc(sig["stat1"], 1)
                    dve.wait_ge(sig["stat1"], n + 1)
                    settle(dve)
                    v.bn_aggr(mv1[:, :], st1[:, :]).then_inc(sig["mean1"], 1)
                rowmax(1)
                if has(b, 2):
                    dve.wait_ge(sig["rstd1"], n + 1)
                    if due(n):
                        dve.wait_ge(sig["qrem"], n)
                    v.tensor_scalar(n1[:, :, :].rearrange("p (g k) d -> p k g d", g=G),
                                    xq[:, u, :].rearrange("p (k g d) -> p k g d", k=KV, g=G),
                                    mv1[:, 0:1], rs1[:, :], ALU.subtract, ALU.mult).then_inc(sig["n1_ready"], 1)
                if has(b, -1):
                    result(b - 1, 1)
                    dve.wait_ge(sig["o_free"], 2 * b)
                    dve.wait_ge(xr_in[o], 16 * (h + u))
                    if due(16 * (h + u - 1)):
                        dve.wait_ge(x2_st[o], 16 * (h + u - 1))
                    v.tensor_tensor(x2[:, o, :], at[:, :, :].rearrange("p h d -> p (h d)"), xr[:, o, :],
                                    ALU.add).then_inc(sig["x2_ready"], 1)
                rowmax(2)
                if has(b, -1):
                    dve.wait_ge(sig["x2_ready"], b)
                    v.bn_stats(st2[:, :], x2[:, o, :]).then_inc(sig["stat2"], 1)
                    dve.wait_ge(sig["stat2"], b)
                    settle(dve)
                    v.bn_aggr(mv2[:, :], st2[:, :]).then_inc(sig["mean2"], 1)
                if has(b, -2):
                    c = b - 2
                    dve.wait_ge(sig["pos"], c + 1)
                    v.tensor_tensor(pp[:, :, :], oh[:, :, :], ps[:, DB, 0:NEXP].unsqueeze(1).broadcast_to([P, TOPK, NEXP]),
                                    ALU.mult).then_inc(sig["pp_ready"], 1)
                    dve.wait_ge(sig["pp_ready"], c + 1)
                    v.tensor_reduce(pk[:, :], pp[:, :, :], X, ALU.add).then_inc(sig["pk_ready"], 1)
                if has(b, -1):
                    dve.wait_ge(sig["rstd2"], b)
                    if due(16 * (h + u - 1)):
                        dve.wait_ge(n2_st[o], 16 * (h + u - 1))
                    v.tensor_scalar(n2[:, o, :], x2[:, o, :], mv2[:, 0:1], rs2[:, :], ALU.subtract,
                                    ALU.mult).then_inc(sig["n2_ready"], 1)
                rowmax(3)
                if has(b, 2):
                    dve.wait_ge(sig["qcopy0"], n + 1)
                    if due(n):
                        dve.wait_ge(sig["qs_ready"], n)
                    v.tensor_tensor(rem[:, :, :], n1[:, :, :], qs[:, :, 0:DH], ALU.subtract).then_inc(sig["qrem"], 1)
                if has(b, -2):
                    dve.wait_ge(sig["pk_ready"], c + 1)
                    v.tensor_scalar(va[:, :], pk[:, :], float(CAP), None, ALU.is_lt).then_inc(sig["va_ready"], 1)
                    v.scalar_tensor_tensor(sl0[:, :], ixf[:, :, 0], float(CAP), pk[:, :], ALU.mult,
                                           ALU.add).then_inc(sig["sl0_ready"], 1)
                    dve.wait_ge(sig["sl0_ready"], c + 1)
                    if due(c):
                        dve.wait_ge(sig["trc_ready"], c)
                    v.tensor_tensor(sl1[:, :], sl0[:, :], trc[:, :], ALU.subtract).then_inc(sig["sl1_ready"], 1)
                    dve.wait_ge(sig["sl1_ready"], c + 1)
                    v.tensor_tensor(sl2[:, :], sl1[:, :], va[:, :], ALU.mult).then_inc(sig["sl2_ready"], 1)
                    dve.wait_ge(sig["sl2_ready"], c + 1)
                    if due(16 * TOPK * (h - 1)):
                        dve.wait_ge(pair_st[u], 16 * TOPK * (h - 1))
                    v.tensor_tensor(slot[:, u, :], sl2[:, :], trc[:, :], ALU.add).then_inc(sig["slot_ready"], 1)
                    dve.wait_ge(sig["slot_ready"], c + 1)
                    v.tensor_scalar(trc[:, :], trc[:, :], float(P), None, ALU.add).then_inc(sig["trc_ready"], 1)
                rowmax(4)
                rowmax(5)
                if has(b, -1):
                    c = b - 1
                    dve.wait_ge(sig["lg"], c + 1)
                    v.tensor_reduce(nlm[:, :], ps[:, DB, 0:NEXP], X, ALU.max, negate=True).then_inc(sig["lgmax"], 1)
                if has(b, 2):
                    dve.wait_ge(sig["qcopy1"], n + 1)
                    v.tensor_tensor(qs[:, :, 5 * DH:6 * DH], rem[:, :, :], qs[:, :, 3 * DH:4 * DH],
                                    ALU.subtract).then_inc(sig["qs_ready"], 1)
                rowmax(6)
                if has(b, -1):
                    dve.wait_ge(sig["pexp"], c + 1)
                    v.reciprocal(rz[:, :], zs[:, :]).then_inc(sig["rz_ready"], 1)
                    dve.wait_ge(sig["rz_ready"], c + 1)
                    v.tensor_scalar(sc[:, :], pe_[:, :], rz[:, :], None, ALU.mult).then_inc(sig["sc_ready"], 1)
                    dve.wait_ge(sig["sc_ready"], c + 1)
                    settle(dve)
                    v.max(top[:, :], sc[:, :]).then_inc(sig["top_ready"], 1)
                    dve.wait_ge(sig["top_ready"], c + 1)
                    settle(dve)
                    v.max_index(tix[:, :], top[:, :], sc[:, :]).then_inc(sig["tix_ready"], 1)
                rowmax(7)
                if has(b, 1):
                    dve.wait_ge(sig["rowmax"], KV * (b + 2))
                    if due(b + 1):
                        dve.wait_ge(sig["m_tr"], b + 1)
                    mp = mm[:, :, :].rearrange("p g (i r) -> p g i r", i=2)
                    nv = nm[:, :, :].rearrange("p g (k i) -> p g i k", i=2)
                    v.tensor_copy(mp[:, :, :, 0:KV:2], nv).then_inc(sig["mm_hi"], 1)
                    dve.wait_ge(sig["mm_hi"], b + 2)
                    v.tensor_tensor(mp[:, :, :, 1:KV:2], nv, mp[:, :, :, 0:KV:2],
                                    ALU.subtract).then_inc(sig["mm_ready"], 1)
                if has(b, 0):
                    if due(b):
                        dve.wait_ge(sig["x2_ready"], b)
                    result(b, 0)
                if has(b, -1):
                    dve.wait_ge(sig["tix_ready"], c + 1)
                    v.tensor_copy(ixf[:, :, 0], tix[:, 0:TOPK]).then_inc(sig["ixf_ready"], 1)
                    v.tensor_reduce(s6[:, :], top[:, 0:TOPK], X, ALU.add).then_inc(sig["s6_ready"], 1)
                    dve.wait_ge(sig["ixf_ready"], c + 1)
                    v.tensor_tensor(oh[:, :, :], lane[:, :].unsqueeze(1).broadcast_to([P, TOPK, NEXP]),
                                    ixf[:, :, :].broadcast_to([P, TOPK, NEXP]), ALU.is_equal).then_inc(sig["oh_ready"], 1)
                    dve.wait_ge(sig["s6_ready"], c + 1)
                    v.tensor_scalar(s6e[:, :], s6[:, :], 1e-20, None, ALU.add).then_inc(sig["s6e_ready"], 1)
                    dve.wait_ge(sig["oh_ready"], c + 1)
                    v.tensor_reduce(mk[:, :], oh[:, :, :].rearrange("p k e -> p e k"), X,
                                    ALU.add).then_inc(sig["mk_ready"], 1)
                    dve.wait_ge(sig["s6e_ready"], c + 1)
                    v.reciprocal(r6[:, :], s6e[:, :]).then_inc(sig["r6_ready"], 1)
                    dve.wait_ge(sig["mk_ready"], c + 1)
                    v.tensor_tensor(run[:, u, :], run[:, o, :], mk[:, :], ALU.add).then_inc(sig["run_ready"], 1)
                    dve.wait_ge(sig["r6_ready"], c + 1)
                    if due(16 * TOPK * (h + u - 1)):
                        dve.wait_ge(pair_st[o], 16 * TOPK * (h + u - 1))
                    v.tensor_scalar(dat[:, o, :, 1], top[:, 0:TOPK], r6[:, :], None,
                                    ALU.mult).then_inc(sig["w_ready"], 1)
                    if due(c):
                        dve.wait_ge(sig["tok_ready"], c)
                    v.tensor_copy(dat[:, o, :, 0], tok[:, :].broadcast_to([P, TOPK])).then_inc(sig["ids_ready"], 1)
                    dve.wait_ge(sig["ids_ready"], c + 1)
                    v.tensor_scalar(tok[:, :], tok[:, :], float(P), None, ALU.add).then_inc(sig["tok_ready"], 1)

            steps(dve, step)

            v.memset(wT[:, 0:SH_TILES], 1.0).then_inc(sig["w_init"], 1)
            v.memset(hh[:, :, FF:D], 0.0).then_inc(sig["h_pad"], 1)

            for k in range(2):
                v.tensor_copy(ixg[:, k, :], idsT[:, 4 * k:4 * k + 4]).then_inc(sig["ixg_ready"], 1)

            def tile_list(i):
                if i == 1:
                    dve.wait_ge(sig["cnt"], 1)
                    v.tensor_scalar(cc[:, :], ps[:, LB, 0:NEXP], float(CAP), None, ALU.min).then_inc(sig["cc_ready"], 1)
                    dve.wait_ge(sig["cc_ready"], 1)
                    gt = oh[:, :, :].rearrange("p k e -> p (k e)").rearrange("p (e k) -> p e k", k=CAP_BLOCKS)
                    v.tensor_tensor(gt, cc[:, :].unsqueeze(2).broadcast_to([P, NEXP, CAP_BLOCKS]),
                                    thr[:, :].unsqueeze(1).broadcast_to([P, NEXP, CAP_BLOCKS]),
                                    ALU.is_gt).then_inc(sig["gt_ready"], 1)
                    dve.wait_ge(sig["gt_ready"], 1)
                    v.tensor_reduce(ntl[:, :], gt, X, ALU.add).then_inc(sig["nt_ready"], 1)
                    dve.wait_ge(sig["nt_ready"], 1)
                    v.tensor_tensor_scan(cum[:, :], ones[:, 0:NEXP], ntl[:, :], 0.0, ALU.mult,
                                         ALU.add).then_inc(sig["cum_ready"], 1)
                    dve.wait_ge(sig["cum_ready"], 1)
                    v.tensor_scalar(le[:, 0:NEXP - 1], cum[:, 0:NEXP - 1], jcol[:, :], None,
                                    ALU.is_le).then_inc(sig["le_ready"], 1)
                    dve.wait_ge(sig["le_ready"], 1)
                    v.tensor_reduce(ej[:, :], le[:, 0:NEXP - 1], X, ALU.add).then_inc(sig["ej_ready"], 1)
                if i == 2:
                    v.tensor_tensor(lec[:, 0:NEXP - 1], le[:, 0:NEXP - 1], cum[:, 0:NEXP - 1],
                                    ALU.mult).then_inc(sig["lec_ready"], 1)
                    dve.wait_ge(sig["lec_ready"], 1)
                    v.tensor_reduce(toj[:, :], lec[:, 0:NEXP - 1], X, ALU.max).then_inc(sig["toj_ready"], 1)
                    dve.wait_ge(sig["toj_ready"], 1)
                    v.tensor_tensor(jr[:, :], jcol[:, :], toj[:, :], ALU.subtract).then_inc(sig["jr_ready"], 1)
                    dve.wait_ge(sig["jr_ready"], 1)
                    dve.wait_ge(sig["ej_ready"], 1)
                    v.scalar_tensor_tensor(blk[:, :], ej[:, :], float(CAP_BLOCKS), jr[:, :], ALU.mult,
                                           ALU.add).then_inc(sig["blk_ready"], 1)
                if i == 3:
                    dve.wait_ge(sig["et_mm"], 1)
                    v.tensor_copy(etab[0:1, SH_TILES:TILES], ps[0:1, LB, 0:P]).then_inc(sig["et_ready"], 1)
                if i == 5:
                    dve.wait_ge(sig["idt_tr"], 1)
                    v.tensor_copy(idsT[:, SH_TILES:TILES], ps[:, LB, 0:P]).then_inc(sig["ids_all"], 1)
                    v.tensor_copy(wT[:, SH_TILES:TILES], ps[:, LB, P:2 * P]).then_inc(sig["wt_all"], 1)
                    dve.wait_ge(sig["ids_all"], 1)
                    dve.wait_ge(sig["wt_all"], 1)

            def x_copy(j, r):
                w = r % 2
                dve.wait_ge(sig["x_tr"], j + 1)
                if not isinstance(j, int) or j >= 2:
                    dve.wait_ge(sig["gu"], j - 1)
                v.tensor_copy(xT[:, w, :], ps[:, XB, 0:D]).then_inc(sig["xT_ready"], 1)

            def gated(j, r):
                w = r % 2
                dve.wait_ge(sig["sg_ready"], j + 1)
                if not isinstance(j, int) or j >= 2:
                    dve.wait_ge(sig["h_tr"], j - 1)
                v.tensor_tensor(hh[:, w, 0:FF], sg[:, w, :], ps[:, GB + w, FF:GU], ALU.mult).then_inc(sig["h_ready"], 1)

            def tile(j, m, r):
                if r % 4 == 0:
                    if isinstance(j, int) and j == 0:
                        dve.wait_ge(sig["w_init"], 1)
                    if not isinstance(j, int) or j >= 8:
                        for i in range(4):
                            dve.wait_ge(y_st[i], 32 * m + 16 * (r // 4) - 16)
                    v.tensor_copy(ixa[:, r // 4, :], idsT[:, bass.ds(j, 4)]).then_inc(sig["ixa_ready"], 1)
                    v.tensor_copy(wj[:, r // 4, :], wT[:, bass.ds(j, 4)]).then_inc(sig["ixa_ready"], 1)
                if not isinstance(j, int) or j + 1 < TILES:
                    gated(j + 1, r + 1)
                if isinstance(j, int):
                    tile_list(j)
                if not isinstance(j, int) or j + 2 < TILES:
                    x_copy(j + 2, r)
                if r % 4 == 3 and (not isinstance(j, int) or j + 5 < TILES):
                    dve.wait_ge(sig["x_tr"], j + 1)
                    v.tensor_copy(ixg[:, r // 4, :], idsT[:, bass.ds(j + 5, 4)]).then_inc(sig["ixg_ready"], 1)
            x_copy(0, 0)
            x_copy(1, 1)
            gated(0, 0)
            eights(dve, tile)

            for c in range(FCH):
                dve.wait_ge(f_in[c], 32)
                v.tensor_tensor(fa[:, c, :, :], fa[:, c, :, :], fb[:, c, :, :], ALU.add).then_inc(sig["fin_add"], 1)


def kernel(x, ctx_512, L0_ffn_wg_router, L0_ffn_w_gate, L0_ffn_w_up, L0_ffn_w_down,
           L0_ffn_ws_gate, L0_ffn_ws_up, L0_ffn_ws_down):
    import concourse.bacc as bacc
    from concourse.bass_utils import run_bass_kernel_spmd

    def rows(w):
        return w.reshape(w.shape[0], w.shape[1] // P, P, w.shape[2]).transpose(2, 0, 1, 3)

    a = [np.asarray(v) for v in (L0_ffn_w_gate, L0_ffn_w_up, L0_ffn_w_down, L0_ffn_ws_gate, L0_ffn_ws_up, L0_ffn_ws_down)]
    halves = lambda w: w.reshape(D, NSHARED, FF).transpose(1, 0, 2)
    gate = np.concatenate([a[0], halves(a[3])], axis=0)
    up = np.concatenate([a[1], halves(a[4])], axis=0)
    down = np.concatenate([a[2], a[5].reshape(NSHARED, FF, D)], axis=0)
    arrays = {
        "x": np.ascontiguousarray(x),
        "ctx": np.ascontiguousarray(ctx_512),
        "wrT": np.ascontiguousarray(np.asarray(L0_ffn_wg_router).T.reshape(2, P, NEXP).transpose(1, 0, 2)),
        "wgu": np.ascontiguousarray(np.concatenate([rows(gate), rows(up)], axis=3)),
        "wdn0": np.ascontiguousarray(down[:, :F0].transpose(1, 0, 2)),
        "wdn1": np.ascontiguousarray(down[:, F0:].transpose(1, 0, 2)),
    }
    nc = bacc.Bacc("TRN2", target_bir_lowering=False, num_devices=1)
    args = {n: nc.dram_tensor(n, v.shape, mybir.dt.from_np(v.dtype), kind="ExternalInput").ap() for n, v in arrays.items()}
    out = nc.dram_tensor("out", (B, S, D), F32, kind="ExternalOutput").ap()
    build(nc, out=out, **args)
    r = run_bass_kernel_spmd(nc, [arrays], core_ids=[0])
    return r.results[0]["out"]
```

```python
from contextlib import ExitStack

import numpy as np
import concourse.bass as bass
from concourse import mybir

F32 = mybir.dt.float32
BF16 = mybir.dt.bfloat16
U32 = mybir.dt.uint32
I32 = mybir.dt.int32
ALU = mybir.AluOpType
ACT = mybir.ActivationFunctionType
X = mybir.AxisListType.X

P = 128
B, S, D = 16, 128, 256
T = B * S
KV, G, DH = 8, 4, 8
HEADS = KV * G
NEXP, TOPK, FF = 32, 6, 176
CAP = 2 * (T * TOPK // NEXP)
CAP_BLOCKS = CAP // P
PARTS = 6
KROWS = PARTS * DH
KPAD = 64
VPAD = 32
KH = KV // 2
SCALE = float(1.0 / np.sqrt(np.float32(DH)))
LN_EPS = 1e-5
NSHARED = 2
NE2 = NEXP + NSHARED
SH_TILES = NSHARED * B
MOE_TILES = (T * TOPK) // P + NEXP
BLOCKS = (NEXP - 1) * CAP_BLOCKS + MOE_TILES
ROWS = BLOCKS * P
TRASH = ROWS
PADROWS = T + P
GU = 2 * FF
F0, F1 = P, FF - P
FCH = 4
CCE_MAX = 2048


def build(nc, x, ctx, wrT, wgu, wdn0, wdn1, out):
    n2_d = nc.dram_tensor("n2_rows", (PADROWS, D), F32, kind="Internal").ap()
    acc_d = [out.rearrange("b s d -> (b s) d"), nc.dram_tensor("acc1", (T, D), F32, kind="Internal").ap()]
    n2T_d = nc.dram_tensor("n2_transposed", (B, P, 2, P), F32, kind="Internal").ap()
    tab_d = nc.dram_tensor("pair_table", (ROWS + TOPK * T, 2), F32, kind="Internal").ap()
    es = ExitStack()
    with es:
        def sb(name, shape, dt=F32):
            return es.enter_context(nc.sbuf_tensor(name, shape, dt))

        def sem(name):
            return es.enter_context(nc.semaphore(name))

        wgu_s = sb("wgu_s", [P, NE2, 2, GU])
        wdn0_s = sb("wdn0_s", [P, NE2, D])
        wdn1_s = sb("wdn1_s", [F1, NE2, D])
        wr_s = sb("wr_s", [P, 2, NEXP])
        idf = sb("idf", [P, P])
        idb = sb("idb", [P, P], BF16)
        ones = sb("ones", [P, P])
        before = sb("before", [P, P])
        kvsel = sb("kvsel", [P, KV, P], BF16)
        lane = sb("lane", [P, NEXP])
        neghalf = sb("neghalf", [P, 1])
        jcol = sb("jcol", [P, 1])
        thr = sb("thr", [P, CAP_BLOCKS])
        xq = sb("xq", [P, 2, D])
        xr = sb("xr", [P, 2, D])
        cb = sb("cb", [P, 2, KV * DH])
        hT = sb("n1_rem_or_hT", [P, 2, D])
        n1, rem = [hT[:, i, :].rearrange("p (h d) -> p h d", d=DH) for i in range(2)]
        krem = sb("krem", [P, KV, DH])
        qs = sb("qs", [P, HEADS, KPAD], BF16)
        ks = sb("ks", [P, KV, KPAD], BF16)
        vx = sb("vx", [P, 2, KV, VPAD])
        OT = sb("OT", [P, G * S])
        arena = sb("qT_or_xg_yy", [P, 8, D])
        qT = arena[:, :, :].rearrange("p a d -> p (a d)").bitcast(BF16).rearrange(
            "p (u k s) -> p u k s", u=2, k=KV // 2)
        xg, yy = arena[:, 0:4, :], arena[:, 4:8, :]
        kT = sb("kT", [P, 2, KV, S], BF16)
        nm = sb("nm", [P, G, KV])
        mm = sb("mm", [P, G, P], BF16)
        mT = sb("mT", [P, G * S], BF16)
        prx = sb("pr_or_xT_sg", [P, 2 * G * S])
        pr = prx[:, :].rearrange("p (u s) -> p u s", u=2)
        xT = prx[:, 0:2 * D].rearrange("p (u d) -> p u d", u=2)
        sg = prx[:, 2 * D:2 * D + 2 * FF].rearrange("p (u d) -> p u d", u=2)
        st1 = sb("st1", [P, 6])
        mv1 = sb("mv1", [P, 2])
        ve1 = sb("ve1", [P, 1])
        rs1 = sb("rs1", [P, 1])
        nb1 = sb("nb1", [P, 1])
        st2 = sb("st2", [P, 6])
        mv2 = sb("mv2", [P, 2])
        ve2 = sb("ve2", [P, 1])
        rs2 = sb("rs2", [P, 1])
        nb2 = sb("nb2", [P, 1])
        den = sb("den", [P, 2, KH, G, 1])
        hh = sb("at_n2T_or_h", [P, 2, D])
        at = hh[:, 0, :].rearrange("p (h d) -> p h d", d=DH)
        n2T = hh[:, 1, :].rearrange("p (c t) -> p c t", c=2)
        x2 = sb("x2", [P, D])
        n2 = sb("n2", [P, D])
        nlm = sb("nlm", [P, 1])
        pe_ = sb("pe_", [P, NEXP])
        zs = sb("zs", [P, 1])
        rz = sb("rz", [P, 1])
        sc = sb("sc", [P, NEXP])
        top = sb("top", [P, 8])
        tix = sb("tix", [P, 8], U32)
        s6 = sb("s6", [P, 1])
        s6e = sb("s6e", [P, 1])
        r6 = sb("r6", [P, 1])
        ixf = sb("ixf", [P, TOPK, 1])
        oh = sb("oh", [P, TOPK, NEXP])
        mk = sb("mk", [P, NEXP])
        run = sb("run", [P, 2, NEXP])
        pp = sb("pp", [P, TOPK, NEXP])
        pk = sb("pk", [P, TOPK])
        va = sb("va", [P, TOPK])
        sl0 = sb("sl0", [P, TOPK])
        sl1 = sb("sl1", [P, TOPK])
        sl2 = sb("sl2", [P, TOPK])
        tok = sb("tok", [P, 1])
        trc = sb("trc", [P, TOPK])
        slot = sb("slot", [P, 2, TOPK], U32)
        dat = sb("dat", [P, 2, TOPK, 2])
        idsT = sb("idsT", [P, MOE_TILES + 8])
        qsf = qs[:, :, :].rearrange("p h k -> p (h k)").bitcast(F32)
        wT = qsf[:, 0:MOE_TILES + 8]
        etab = qsf[0:1, MOE_TILES + 8:2 * (MOE_TILES + 8)].bitcast(I32)
        ixg = sb("ixg", [P, 2, 4], U32)
        ixa = sb("ixa", [P, 2, 4], U32)
        wj = sb("wj", [P, 2, 4])
        init = xg.rearrange("p a d -> p (a d)")[:, 0:2 * BLOCKS].rearrange(
            "p (r c) -> p r c", c=2)
        initi = yy.rearrange("p a d -> p (a d)")[:, 0:BLOCKS].bitcast(I32)
        zero = yy[:, 2, :]
        blk = sb("blk", [P, 1], U32)
        ej = sb("ej", [P, 1])
        toj = sb("toj", [P, 1])
        jr = sb("jr", [P, 1])
        cum, ntl, cc, le, lec = [OT[:, i * NEXP:(i + 1) * NEXP] for i in range(5)]
        g2 = x2[:, :].rearrange("p (r c) -> p r c", c=2)
        ps = es.enter_context(nc.psum_tensor("ps", [P, 8, 512], F32))
        psb = ps[:, :, :].bitcast(BF16)
        SM, SE, CQ, OB, DB = 0, 2, 4, 5, 7
        XB, LB, GB, HB, YB = 0, 1, 2, 4, 6

        names = """held const_pool const_sel const_dve init_iota init_and init_add init_zero init_done wr_in ws_in w_in nt_st
        kc0 kc1 kc2 kc3 ks_ready vx_ready stat1 mean1 veps1 rstd1 nb1_ready n1_ready qcopy0 qrem qcopy1 qs_ready
        q_tr k_tr m_tr q_ev k_ev m_ev s1 s2 pv rowmax mm_hi mm_ready expd
        o_ev o_tr den_ready o_free x2_ready stat2 mean2 veps2 rstd2 nb2_ready n2_ready n2_tr n2_ev lg lgmax pexp
        rz_ready sc_ready top_ready tix_ready s6_ready s6e_ready r6_ready w_ready ixf_ready
        oh_ready mk_ready run_ready pos pp_ready pk_ready va_ready sl0_ready sl1_ready sl2_ready slot_ready ids_ready
        tok_ready trc_ready cnt cc_ready gt_ready nt_ready cum_ready le_ready ej_ready lec_ready toj_ready jr_ready
        blk_ready h_pad g2_in et_mm et_ready idt_tr ids_all wt_all
        ixg_ready ixa_ready x_tr xT_ready gu sg_ready h_ready h_tr hT_ready dn y_ready
       """.split()
        sig = {n: sem(n) for n in names}
        xq_in = [sem(f"xq_in{i}") for i in range(2)]
        xr_in = [sem(f"xr_in{i}") for i in range(2)]
        c_in = [sem(f"c_in{i}") for i in range(2)]
        ys_st = [sem(f"ys_st{i}") for i in range(4)]
        xs_in = [sem(f"xs_in{i}") for i in range(2)]
        x2_st, n2_st = sem("x2_st"), sem("n2_st")
        pair_st = [sem(f"pair_st{i}") for i in range(2)]
        g_in = [sem(f"g_in{i}") for i in range(4)]
        y_st = [sem(f"y_st{i}") for i in range(4)]
        f_st = sem("f_st")
        NCONST_POOL = 8

        block = es.enter_context(nc.Block())

        def due(n):
            return not isinstance(n, int) or n > 0

        def settle(eng):
            eng.sem_inc(sig["held"], 1)

        def steps(eng, step):
            for b in range(-3, 2):
                step(b, b // 2, b % 2)
            with eng.Fori(1, B // 2 - 2) as h:
                for u in range(2):
                    step(2 * h + u, h, u)
            for b in range(B - 4, B + 2):
                step(b, b // 2, b % 2)

        def has(b, off):
            return not isinstance(b, int) or 0 <= b + off < B

        AHEAD = 4

        def tiles(eng, tile, first=0):
            for shared, count in ((True, SH_TILES), (False, MOE_TILES)):
                for r in range(first if shared else 0, 8):
                    tile(r, 0, r, shared)
                with eng.Fori(1, count // 8 - 1) as m:
                    for r in range(8):
                        tile(8 * m + r, m, r, shared)
                for r in range(8):
                    tile(count - 8 + r, count // 8 - 1, r, shared)

        def later(i, m, r, shared, k):
            if isinstance(i, int):
                if shared and i + k >= SH_TILES:
                    i, shared = i + k - SH_TILES, False
                else:
                    i = i + k
                return (i, i // 8, i % 8, shared) if i < MOE_TILES else None
            return (i + k, m + (r + k) // 8, (r + k) % 8, shared)

        def nth(i, shared):
            return i + 1 if shared else i + 1 + SH_TILES

        @block.sync
        def _(sp):
            def load_x(b, u):
                sp.dma_start(xq[:, u, :], x[bass.ds(b, 1), :, :].rearrange("a p d -> p (a d)")).then_inc(xq_in[u], 16)

            def load_c(b, u):
                sp.dma_start(cb[:, u, :], ctx[bass.ds(b, 1), :, :].rearrange("a p d -> p (a d)")).then_inc(c_in[u], 16)

            def load_xT(s, w):
                sp.dma_start(xT[:, w, :].rearrange("p (c t) -> p c t", c=2),
                             n2T_d[bass.ds(s, 1), :, :, :].rearrange("a p c t -> p (a c) t")).then_inc(xs_in[w], 16)

            def load_r(b, u):
                sp.dma_start(xr[:, u, :], x[bass.ds(b, 1), :, :].rearrange("a p d -> p (a d)")).then_inc(xr_in[u], 16)

            load_x(0, 0)
            load_c(0, 0)
            load_x(1, 1)
            load_c(1, 1)
            sp.dma_start(wr_s[:, :, :], wrT).then_inc(sig["wr_in"], 16)
            sp.wait_ge(sig["init_zero"], 1)
            sp.dma_start(n2_d[T:PADROWS, :], zero).then_inc(sig["init_done"], 16)
            sp.wait_ge(sig["init_add"], 2)
            sp.dma_start(tab_d[0:ROWS, :].rearrange("(p r) c -> p r c", p=P), init).then_inc(sig["init_done"], 16)

            e = NEXP
            sp.dma_start(wgu_s[:, e:, :, :], wgu[:, e:, :, :]).then_inc(sig["ws_in"], 16)
            sp.dma_start(wdn0_s[:, e:, :], wdn0[:, e:, :]).then_inc(sig["ws_in"], 16)
            sp.dma_start(wdn1_s[:, e:, :], wdn1[:, e:, :]).then_inc(sig["ws_in"], 16)

            def step(b, h, u):
                o = 1 - u
                if has(b, -1):
                    if due(b):
                        sp.wait_ge(sig["x2_ready"], b)
                    sp.dma_start(acc_d[0][bass.ds((b - 1) * P, P), :], x2[:, :]).then_inc(x2_st, 16)
                if has(b, 1):
                    load_r(b + 1, o)
                if has(b, -1):
                    if due(b):
                        sp.wait_ge(sig["n2_ready"], b)
                    sp.dma_start(n2_d[bass.ds((b - 1) * P, P), :], n2[:, :]).then_inc(n2_st, 16)
                if has(b, 0):
                    e = 2 * b
                    sp.dma_start(wgu_s[:, bass.ds(e, 2), :, :], wgu[:, bass.ds(e, 2), :, :]).then_inc(sig["w_in"], 16)
                    sp.dma_start(wdn0_s[:, bass.ds(e, 2), :], wdn0[:, bass.ds(e, 2), :]).then_inc(sig["w_in"], 16)
                    sp.dma_start(wdn1_s[:, bass.ds(e, 2), :], wdn1[:, bass.ds(e, 2), :]).then_inc(sig["w_in"], 16)
                if has(b, 4) and has(b, 2):
                    sp.wait_ge(sig["n1_ready"], b + 3)
                    load_x(b + 4, u)
                if has(b, 3) and has(b, 1):
                    sp.wait_ge(sig["vx_ready"], b + 2)
                    load_c(b + 3, o)
                if has(b, -1):
                    sp.wait_ge(sig["n2_ev"], b)
                    sp.dma_start(n2T_d[bass.ds(b - 1, 1), :, :, :].rearrange("a p c t -> p (a c) t"), n2T).then_inc(sig["nt_st"], 16)
                if isinstance(b, int) and b == B - 1:
                    sp.wait_ge(sig["pv"], KV * B)
                    sp.wait_ge(sig["nt_st"], 16 * (B - 1))
                    load_xT(0, 0)
                    load_xT(1, 1)

            steps(sp, step)

            sp.wait_ge(sig["nt_st"], 16 * B)

            def sequence(s, i):
                if not isinstance(s, int) or s + 2 < B:
                    sp.wait_ge(sig["gu"], 2 * s + 2)
                    load_xT(s + 2, i % 2)
                sp.wait_ge(sig["y_ready"], s + 1)
                sp.dma_start(acc_d[1][bass.ds(s * P, P), :], yy[:, i, :]).then_inc(ys_st[i], 16)

            with sp.Fori(0, B // 4 - 1) as m:
                for i in range(4):
                    sequence(4 * m + i, i)
            for i in range(4):
                sequence(B - 4 + i, i)

        @block.gpsimd
        def _(pool):
            g = nc.gpsimd
            cp = sig["const_pool"]
            g.memset(idf[:, :], 0.0).then_inc(cp, 1)
            g.memset(idb[:, :], 0.0).then_inc(cp, 1)
            g.memset(before[:, :], 1.0).then_inc(cp, 1)
            g.memset(vx[:, :, :, :], 0.0).then_inc(cp, 1)
            g.iota(initi, [[1, BLOCKS]], base=0, channel_multiplier=BLOCKS % P).then_inc(sig["init_iota"], 1)
            pool.wait_ge(cp, 4)
            for m in (idf, idb):
                g.affine_select(out=m[:, :], in_=m[:, :], compare_op=ALU.not_equal, fill=1.0, base=0,
                                pattern=[[-1, P]], channel_multiplier=1).then_inc(cp, 1)
            g.affine_select(out=before[:, :], in_=before[:, :], compare_op=ALU.is_gt, fill=0.0, base=0,
                            pattern=[[1, P]], channel_multiplier=-1).then_inc(cp, 1)
            g.iota(lane[:, :], [[1, NEXP]], base=0, channel_multiplier=0, allow_small_or_imprecise_dtypes=True)
            g.iota(jcol[:, :], [[1, 1]], base=0, channel_multiplier=1, allow_small_or_imprecise_dtypes=True)
            g.iota(thr[:, :], [[P, CAP_BLOCKS]], base=0, channel_multiplier=0, allow_small_or_imprecise_dtypes=True)
            g.iota(tok[:, :], [[1, 1]], base=0, channel_multiplier=1, allow_small_or_imprecise_dtypes=True)
            g.iota(trc[:, :], [[T, TOPK]], base=TRASH, channel_multiplier=1, allow_small_or_imprecise_dtypes=True)
            g.memset(neghalf[:, :], -0.5)
            g.memset(vx[:, :, :, DH:DH + 1], 1.0).then_inc(cp, 1)

            def selector():
                cs = sig["const_sel"]
                g.memset(kvsel[:, :, :], 1.0).then_inc(cs, 1)
                ksv = kvsel[:, :, :].rearrange("p (a b) c -> p a b c", b=2)
                pool.wait_ge(cs, 1)
                g.affine_select(out=ksv, in_=ksv, compare_op=ALU.is_ge, fill=0.0, base=0,
                                pattern=[[-2, KV // 2], [-KPAD, 2], [0, P]], channel_multiplier=1).then_inc(cs, 1)
                pool.wait_ge(cs, 2)
                g.affine_select(out=ksv, in_=ksv, compare_op=ALU.is_ge, fill=0.0, base=1,
                                pattern=[[2, KV // 2], [KPAD, 2], [0, P]], channel_multiplier=-1).then_inc(cs, 1)

            def scatter(c, u):
                pool.wait_ge(sig["slot_ready"], c + 1)
                pool.wait_ge(sig["ids_ready"], c + 1)
                if isinstance(c, int) and c == 0:
                    pool.wait_ge(sig["init_done"], 16 * 2)
                settle(pool)
                for k in range(TOPK):
                    g.indirect_dma_start(tab_d, bass.IndirectOffsetOnAxis(ap=slot[:, u, k:k + 1], axis=0),
                                         dat[:, u, k, :], None).then_inc(pair_st[u], 16)

            def scale_bias(mv, ve, rs, nb, s0, s1, s2, n):
                settle(pool)
                g.tensor_scalar(ve[:, :], mv[:, 1:2], LN_EPS, None, ALU.add).then_inc(s0, 1)
                pool.wait_ge(s0, n)
                g.tensor_tensor(rs[:, :], ve[:, :], neghalf[:, :], ALU.pow).then_inc(s1, 1)
                pool.wait_ge(s1, n)
                settle(pool)
                g.tensor_scalar(nb[:, :], mv[:, 0:1], rs[:, :], -1.0, ALU.mult, ALU.mult).then_inc(s2, 1)

            def step(b, h, u):
                o = 1 - u
                if has(b, -1):
                    pool.wait_ge(sig["mean2"], b)
                    if due(b - 1):
                        pool.wait_ge(sig["n2_ready"], b - 1)
                    scale_bias(mv2, ve2, rs2, nb2, sig["veps2"], sig["rstd2"], sig["nb2_ready"], b)
                if has(b, 2):
                    n = b + 2
                    pool.wait_ge(c_in[u], 16 * (h + 2))
                    if due(n):
                        pool.wait_ge(sig["k_tr"], n)
                    c3 = cb[:, u, :].rearrange("p (k d) -> p k d", d=DH)
                    kv4 = ks[:, :, 0:KROWS].rearrange("p k (j d) -> p k j d", d=DH)
                    kj = [kv4[:, :, j, :] for j in range(PARTS)]
                    settle(pool)
                    g.tensor_copy(kj[0], c3).then_inc(sig["kc0"], 1)
                    g.tensor_copy(kj[3], c3)
                    g.tensor_copy(kj[5], c3)
                    pool.wait_ge(sig["kc0"], n + 1)
                    g.tensor_tensor(krem[:, :, :], c3, kj[0], ALU.subtract).then_inc(sig["kc1"], 1)
                    pool.wait_ge(sig["kc1"], n + 1)
                    settle(pool)
                    g.tensor_copy(kj[1], krem[:, :, :]).then_inc(sig["kc2"], 1)
                    g.tensor_copy(kj[4], krem[:, :, :])
                    pool.wait_ge(sig["kc2"], n + 1)
                    g.tensor_tensor(kj[2], krem[:, :, :], kj[1], ALU.subtract).then_inc(sig["ks_ready"], 1)
                if has(b, 1):
                    if due(KV * b):
                        pool.wait_ge(sig["pv"], KV * b)
                    settle(pool)
                    g.tensor_copy(vx[:, o, :, 0:DH], cb[:, o, :].rearrange("p (k d) -> p k d", d=DH)
                                  ).then_inc(sig["vx_ready"], 1)
                if has(b, 3):
                    pool.wait_ge(sig["mean1"], b + 4)
                    if due(b + 3):
                        pool.wait_ge(sig["n1_ready"], b + 3)
                    scale_bias(mv1, ve1, rs1, nb1, sig["veps1"], sig["rstd1"], sig["nb1_ready"], b + 4)
                if isinstance(b, int) and b == -2:
                    selector()
                if has(b, -2) and not (isinstance(b, int) and b == B - 1):
                    if isinstance(b, int) and b == B:
                        scatter(b - 3, o)
                    scatter(b - 2, u)

            steps(pool, step)

            def gather(i, m, r):
                if r % 4 == 0:
                    pool.wait_ge(sig["ixg_ready"], 2 * m + r // 4 + 1)
                if not isinstance(i, int) or i >= 4:
                    pool.wait_ge(sig["x_tr"], i - 3)
                settle(pool)
                g.indirect_dma_start(xg[:, r % 4, :], None, n2_d,
                                     bass.IndirectOffsetOnAxis(ap=ixg[:, r // 4, r % 4:r % 4 + 1], axis=0)
                                     ).then_inc(g_in[r % 4], 16)

            def add(i, m, r):
                pool.wait_ge(sig["y_ready"], i + 1 + B)
                if r % 4 == 0:
                    pool.wait_ge(sig["ixa_ready"], 4 * m + 2 * (r // 4) + 2)
                if r >= 2:
                    pool.wait_ge(y_st[(r - 2) % 4], 32 * m + 16 * ((r - 2) // 4 + 1))
                elif not isinstance(m, int) or m > 0:
                    pool.wait_ge(y_st[r + 2], 32 * m)
                settle(pool)
                g.indirect_dma_start(acc_d[r % 2], bass.IndirectOffsetOnAxis(ap=ixa[:, r // 4, r % 4:r % 4 + 1], axis=0),
                                     yy[:, r % 4, :], None, bounds_check=T - 1, oob_is_err=False,
                                     compute_op=ALU.add).then_inc(y_st[r % 4], 16)

            pool.wait_ge(sig["blk_ready"], 1)
            for i in range(2):
                pool.wait_ge(pair_st[i], 16 * TOPK * (B // 2))
            pool.wait_ge(x2_st, 16 * B)
            g.indirect_dma_start(x2[:, :], None, tab_d[0:ROWS, :].rearrange("(b r) c -> b (r c)", r=P),
                                 bass.IndirectOffsetOnAxis(ap=blk[:, :], axis=0)).then_inc(sig["g2_in"], 16)
            pool.wait_ge(n2_st, 16 * B)
            for i in range(AHEAD):
                gather(i, 0, i)
            for i in range(4):
                pool.wait_ge(ys_st[i], 16 * (B // 4))

            def tile(i, m, r):
                if not isinstance(i, int) or i + AHEAD < MOE_TILES:
                    gather(i + AHEAD, m + (r + AHEAD) // 8, (r + AHEAD) % 8)
                add(i, m, r)

            for r in range(8):
                tile(r, 0, r)
            with pool.Fori(1, MOE_TILES // 8 - 1) as m:
                for r in range(8):
                    tile(8 * m + r, m, r)
            for r in range(8):
                tile(MOE_TILES - 8 + r, MOE_TILES // 8 - 1, r)
            for i in range(4):
                pool.wait_ge(y_st[i], 16 * (MOE_TILES // 4))
            for c in range(FCH):
                rows = slice(c * T // FCH, (c + 1) * T // FCH)
                g.dma_start(acc_d[0][rows, :], acc_d[1][rows, :], accum_op=ALU.add,
                            max_dma_last_dim=4 * CCE_MAX).then_inc(f_st, 16)
            pool.wait_ge(f_st, 16 * FCH)

        @block.scalar
        def _(act):
            a = nc.scalar

            def silu(i, m, r, shared):
                w, n = r % 2, nth(i, shared)
                act.wait_ge(sig["gu"], n)
                if not isinstance(n, int) or n > 2:
                    act.wait_ge(sig["h_ready"], n - 2)
                a.activation(sg[:, w, :], ps[:, GB + w, 0:FF], ACT.Silu).then_inc(sig["sg_ready"], 1)

            def step(b, h, u):
                o = 1 - u
                if has(b, 0):
                    act.wait_ge(sig["m_tr"], b + 1)
                    if due(KV * b):
                        act.wait_ge(sig["s2"], KV * b)
                    a.activation(mT[:, :], psb[:, DB, 0:G * S], ACT.Copy).then_inc(sig["m_ev"], 1)
                if has(b, -1):
                    act.wait_ge(sig["pv"], KV * b)
                    act.wait_ge(sig["o_tr"], 2 * b - 1)
                    a.activation(OT[:, :], ps[:, OB + 1, :], ACT.Copy).then_inc(sig["o_ev"], 1)
                for kv in range(KV):
                    if has(b, 0):
                        n = KV * b + kv
                        act.wait_ge(sig["s2"], n + 1)
                        if due(n - 1):
                            act.wait_ge(sig["pv"], n - 1)
                        a.activation(pr[:, kv % 2, :], ps[:, SE + kv % 2, :], ACT.Exp,
                                     scale=SCALE).then_inc(sig["expd"], 1)
                    if kv == 0 and has(b, 1):
                        act.wait_ge(sig["q_tr"], 2 * (b + 1) + 2)
                        a.activation(qT[:, o, 2:4, :], psb[:, CQ, :], ACT.Copy).then_inc(sig["q_ev"], 1)
                    if kv == 0 and has(b, 2):
                        act.wait_ge(sig["nb1_ready"], b + 3)
                        if due(b + 2):
                            act.wait_ge(sig["qrem"], b + 2)
                        a.activation(n1[:, :, :].rearrange("p (g k) d -> p k g d", g=G),
                                     xq[:, u, :].rearrange("p (k g d) -> p k g d", k=KV, g=G), ACT.Identity,
                                     bias=nb1[:, :], scale=rs1[:, :]).then_inc(sig["n1_ready"], 1)
                    if kv == 1 and has(b, 2):
                        act.wait_ge(sig["n1_ready"], b + 3)
                        a.activation(qs[:, :, 0:3 * DH].rearrange("p h (j d) -> p h j d", d=DH),
                                     n1.unsqueeze(2).broadcast_to([P, HEADS, 3, DH]),
                                     ACT.Copy).then_inc(sig["qcopy0"], 1)
                    if kv == 4 and has(b, -1):
                        act.wait_ge(sig["nb2_ready"], b)
                        if due(16 * (b - 1)):
                            act.wait_ge(n2_st, 16 * (b - 1))
                        a.activation(n2[:, :], x2[:, :], ACT.Identity, bias=nb2[:, :],
                                     scale=rs2[:, :]).then_inc(sig["n2_ready"], 1)
                    if kv == 4 and has(b, 2):
                        act.wait_ge(sig["qrem"], b + 3)
                        a.activation(qs[:, :, 3 * DH:5 * DH].rearrange("p h (j d) -> p h j d", d=DH),
                                     rem.unsqueeze(2).broadcast_to([P, HEADS, 2, DH]),
                                     ACT.Copy).then_inc(sig["qcopy1"], 1)
                    if kv == 5 and has(b, 0):
                        act.wait_ge(sig["pv"], KV * b + KH)
                        if due(2 * b):
                            act.wait_ge(sig["o_tr"], 2 * b)
                        a.activation(OT[:, :], ps[:, OB, :], ACT.Copy).then_inc(sig["o_ev"], 1)
                    if kv == 5 and has(b, -1):
                        act.wait_ge(sig["n2_tr"], b)
                        if due(b - 1):
                            act.wait_ge(sig["lg"], b - 1)
                            act.wait_ge(sig["nt_st"], 16 * (b - 1))
                        a.activation(n2T[:, :, :], ps[:, DB, 0:D], ACT.Copy).then_inc(sig["n2_ev"], 1)
                    if kv == 5 and has(b, 2):
                        act.wait_ge(sig["q_tr"], 2 * (b + 2) + 1)
                        if isinstance(b, int) and b == -2:
                            act.wait_ge(sig["init_done"], 16 * 2)
                        a.activation(qT[:, u, 0:2, :], psb[:, CQ, :], ACT.Copy).then_inc(sig["q_ev"], 1)
                    if kv == 6 and has(b, -1):
                        act.wait_ge(sig["lgmax"], b)
                        a.activation(pe_[:, :], ps[:, DB, 0:NEXP], ACT.Exp, bias=nlm[:, :],
                                     accum_out=zs[:, :]).then_inc(sig["pexp"], 1)
                    if kv == 6 and has(b, 2):
                        act.wait_ge(sig["k_tr"], b + 3)
                        a.activation(kT[0:KPAD, u, 0:KV:2, :], psb[0:KPAD, CQ, 0:KV // 2 * S].rearrange("p (k s) -> p k s", s=S),
                                     ACT.Copy)
                    if kv == 7 and has(b, 2):
                        a.activation(kT[KPAD:P, u, 1:KV:2, :], psb[KPAD:P, CQ, 0:KV // 2 * S].rearrange("p (k s) -> p k s", s=S),
                                     ACT.Copy).then_inc(sig["k_ev"], 1)
                    if kv == 6 and isinstance(b, int) and b == B:
                        silu(0, 0, 0, True)

            steps(act, step)

            def result(i, m, r, shared):
                if shared:
                    q = r // 2
                    act.wait_ge(sig["dn"], i + 1)
                    if not isinstance(m, int) or m > 0:
                        act.wait_ge(ys_st[q], 16 * m)
                    a.activation(yy[:, q, :], ps[:, YB + q % 2, 0:D], ACT.Copy).then_inc(sig["y_ready"], 1)
                    return
                act.wait_ge(sig["dn"], nth(i, shared))
                if r % 4 == 0:
                    act.wait_ge(sig["ixa_ready"], 4 * m + 2 * (r // 4) + 2)
                if not isinstance(i, int) or i >= 4:
                    act.wait_ge(y_st[r % 4], 32 * m + 16 * (r // 4))
                else:
                    act.wait_ge(ys_st[i], 16 * (B // 4))
                a.activation(yy[:, r % 4, :], ps[:, YB + r % 2, 0:D], ACT.Copy,
                             scale=wj[:, r // 4, r % 4:r % 4 + 1]).then_inc(sig["y_ready"], 1)

            def tile(i, m, r, shared):
                w, n = r % 2, nth(i, shared)
                act.wait_ge(sig["h_tr"], n)
                if not isinstance(n, int) or n > 2:
                    act.wait_ge(sig["dn"], n - 2)
                a.activation(hT[:, w, :], ps[:, HB + w, 0:D], ACT.Copy).then_inc(sig["hT_ready"], 1)
                nx = later(i, m, r, shared, 1)
                if nx:
                    silu(*nx)
                if not shared or r % 2 == 1:
                    result(i, m, r, shared)
            tiles(act, tile)

        @block.tensor
        def _(pe):
            t = nc.tensor
            pe.wait_ge(sig["const_pool"], NCONST_POOL)
            pe.wait_ge(sig["const_dve"], 1)

            def q_transposes(b, half):
                for pr_ in range(2):
                    for g in range(G):
                        pair = 2 * half + pr_
                        h0 = g * KV + 2 * pair
                        last = t.transpose(psb[:, CQ, (pr_ * G + g) * S:(pr_ * G + g + 1) * S],
                                           qs[:, h0:h0 + 2, :].rearrange("p h k -> p (h k)"), idb[:, :])
                last.then_inc(sig["q_tr"], 1)

            def x_transpose(i, m, r):
                pe.wait_ge(g_in[r % 4], 32 * m + 16 * (r // 4 + 1))
                for c in range(2):
                    last = t.transpose(ps[:, XB, c * P:(c + 1) * P], xg[:, r % 4, c * P:(c + 1) * P], idf[:, :])
                last.then_inc(sig["x_tr"], 1)

            def expert_of(j):
                return nc.values_load(etab[0:1, bass.ds(j, 1)], engines=(mybir.EngineType.PE,), min_val=0, max_val=NE2 - 1,
                                      skip_runtime_bounds_check_because="a sum of 31 comparisons, or one of the shared halves")

            def gate_up(i, m, r, shared, e):
                w = r % 2
                if shared:
                    x = xT[:, (r // 2) % 2, :]
                    if r % 2 == 0:
                        pe.wait_ge(xs_in[(r // 2) % 2], 32 * m + 16 * (r // 4 + 1))
                else:
                    x = xT[:, w, :]
                    pe.wait_ge(sig["xT_ready"], i + 1)
                for c in range(2):
                    last = t.matmul(ps[:, GB + w, 0:GU], x[:, c * P:(c + 1) * P],
                                    wgu_s[:, bass.ds(e, 1), c, :].rearrange("p a f -> p (a f)"),
                                    start=(c == 0), stop=(c == 1))
                last.then_inc(sig["gu"], 1)

            def tile_list(i):
                if i == 1:
                    pe.wait_ge(sig["run_ready"], B)
                    t.matmul(ps[:, LB, 0:NEXP], ones[:, :], run[:, 0, :], start=True, stop=True).then_inc(sig["cnt"], 1)
                if i == 5:
                    pe.wait_ge(sig["ej_ready"], 1)
                    t.matmul(ps[0:1, LB, 0:P], ej[:, :], idf[:, :], start=True, stop=True).then_inc(sig["et_mm"], 1)
                if i == 24:
                    pe.wait_ge(sig["w_in"], 16 * 3 * (NEXP // 2))
                    pe.wait_ge(sig["et_ready"], 1)
                    pe.wait_ge(sig["g2_in"], 16)
                    for c in range(2):
                        last = t.transpose(ps[:, LB, c * P:(c + 1) * P], g2[:, :, c], idf[:, :])
                    last.then_inc(sig["idt_tr"], 1)

            def h_transpose(i, m, r, shared):
                w = r % 2
                if shared and isinstance(i, int) and i < 2:
                    pe.wait_ge(sig["h_pad"], i + 1)
                pe.wait_ge(sig["h_ready"], nth(i, shared))
                for c in range(2):
                    last = t.transpose(ps[:, HB + w, c * P:(c + 1) * P], hh[:, w, c * P:(c + 1) * P], idf[:, :])
                last.then_inc(sig["h_tr"], 1)

            def down(i, m, r, shared, e):
                w, n = r % 2, nth(i, shared)
                bank = YB + (r // 2 % 2 if shared else w)
                first, last_one = (w == 0, w == 1) if shared else (True, True)
                pe.wait_ge(sig["hT_ready"], n)
                if isinstance(n, int) and n == 3:
                    pe.wait_ge(sig["pp_ready"], B)
                t.matmul(ps[:, bank, 0:D], hT[:, w, 0:P],
                         wdn0_s[:, bass.ds(e, 1), :].rearrange("p a f -> p (a f)"), start=first, stop=False)
                t.matmul(ps[:, bank, 0:D], hT[0:F1, w, P:2 * P],
                             wdn1_s[:, bass.ds(e, 1), :].rearrange("p a f -> p (a f)"), start=False, stop=last_one).then_inc(sig["dn"], 1)

            expert = {}

            def tile(i, m, r, shared):
                if shared:
                    if isinstance(i, int):
                        tile_list(i)
                    expert[0] = NEXP + r % 2
                nx, nx2 = later(i, m, r, shared, 1), later(i, m, r, shared, 2)
                if nx:
                    expert[1] = NEXP + (r + 1) % 2 if nx[3] else expert_of(nx[0])
                if not shared and r == 0 and (not isinstance(i, int) or i > 0):
                    expert[0] = expert_of(i)
                h_transpose(i, m, r, shared)
                if nx:
                    gate_up(*nx, expert[1])
                if nx2 and not nx2[3]:
                    x_transpose(*nx2[:3])
                down(i, m, r, shared, expert[0])
                expert[0] = expert[1]

            def key_scores(b, kv, o):
                n = KV * b + kv
                if due(n - 1):
                    pe.wait_ge(sig["rowmax"], n - 1)
                if kv == 0:
                    pe.wait_ge(sig["k_ev"], b + 1)
                if kv == KH:
                    pe.wait_ge(sig["q_ev"], 2 * b + 2)
                for g in range(G):
                    last = t.matmul(ps[:, SM + kv % 2, g * S:(g + 1) * S], qT[:, o, kv // 2, g * S:(g + 1) * S],
                                    kT[:, o, kv, :], start=True, stop=True)
                last.then_inc(sig["s1"], 1)

            def o_transposes(half):
                for g in range(G):
                    last = t.transpose(ps[:, OB + half, g * S:(g + 1) * S], OT[:, g * S:(g + 1) * S], idf[:, :])
                last.then_inc(sig["o_tr"], 1)

            def step(b, h, u):
                o = 1 - u
                if has(b, 0):
                    pe.wait_ge(sig["mm_ready"], b + 1)
                    if due(b - 1):
                        pe.wait_ge(sig["pexp"], b - 1)
                    for g in range(G):
                        last = t.transpose(psb[:, DB, g * S:(g + 1) * S], mm[:, g, :], idb[:, :])
                    last.then_inc(sig["m_tr"], 1)
                if has(b, -1):
                    pv(b - 1, KV - 1, o)
                if isinstance(b, int) and b == B + 1:
                    tile(0, 0, 0, True)
                for kv in range(KV):
                    pair = kv // 2
                    if kv == 0 and has(b, 1):
                        key_scores(b + 1, 0, o)
                    if kv + 1 < KV and has(b, 1):
                        key_scores(b + 1, kv + 1, o)
                    if has(b, 0):
                        n = KV * b + kv
                        if due(n - 1):
                            pe.wait_ge(sig["expd"], n - 1)
                        if kv == 0:
                            pe.wait_ge(sig["m_ev"], b + 1)
                            if isinstance(b, int) and b == 0:
                                pe.wait_ge(sig["const_sel"], 3)
                        t.matmul(ps[:, SE + kv % 2, :], kT[:, u, kv, :], qT[:, u, pair, :],
                                 start=True, stop=False)
                        t.matmul(ps[:, SE + kv % 2, :], kvsel[:, kv, :], mT[:, :],
                                 start=False, stop=True).then_inc(sig["s2"], 1)
                    if kv == 0 and has(b, 1):
                        q_transposes(b + 1, 1)
                    if kv == 0 and has(b, -1):
                        pe.wait_ge(sig["o_ev"], 2 * b)
                        o_transposes(1)
                    if kv == 2 and has(b, -2):
                        pe.wait_ge(sig["mk_ready"], b - 1)
                        if not has(b, 0):
                            pe.wait_ge(sig["pexp"], b - 1)
                        t.matmul(ps[:, DB, 0:NEXP], before[:, :], mk[:, :], start=True, stop=False)
                        t.matmul(ps[:, DB, 0:NEXP], ones[:, :], run[:, u, :],
                                 start=False, stop=True).then_inc(sig["pos"], 1)
                    if kv >= 1 and has(b, 0):
                        pv(b, kv - 1, u)
                    if kv == 5 and has(b, -1):
                        pe.wait_ge(sig["n2_ready"], b)
                        if due(b - 1):
                            pe.wait_ge(sig["pp_ready"], b - 1)
                        for c in range(2):
                            last = t.transpose(ps[:, DB, c * P:(c + 1) * P], n2[:, c * P:(c + 1) * P], idf[:, :])
                        last.then_inc(sig["n2_tr"], 1)
                    if kv == 5 and has(b, 2):
                        pe.wait_ge(sig["qs_ready"], b + 3)
                        if due(2 * (b + 2)):
                            pe.wait_ge(sig["q_ev"], 2 * (b + 2))
                        q_transposes(b + 2, 0)
                    if kv == 6 and has(b, -1):
                        pe.wait_ge(sig["n2_ev"], b)
                        if isinstance(b, int) and b == 1:
                            pe.wait_ge(sig["wr_in"], 16)
                        for c in range(2):
                            last = t.matmul(ps[:, DB, 0:NEXP], n2T[:, c, :], wr_s[:, c, :],
                                            start=(c == 0), stop=(c == 1))
                        last.then_inc(sig["lg"], 1)
                    if kv == 6 and has(b, 0):
                        pe.wait_ge(sig["o_ev"], 2 * b + 1)
                        o_transposes(0)
                    if kv == 6 and has(b, 2):
                        pe.wait_ge(sig["ks_ready"], b + 3)
                        pe.wait_ge(sig["q_ev"], 2 * (b + 2) + 1)
                        for pair in range(KV // 2):
                            last = t.transpose(psb[:, CQ, pair * S:(pair + 1) * S],
                                               ks[:, 2 * pair:2 * pair + 2, :].rearrange("p h k -> p (h k)"), idb[:, :])
                        last.then_inc(sig["k_tr"], 1)
                    if kv == 6 and isinstance(b, int) and b == B:
                        pe.wait_ge(sig["ws_in"], 16 * 3)
                        gate_up(0, 0, 0, True, NEXP)

            def pv(b, kv, u):
                half, p0 = kv // KH, VPAD * (kv % KH)
                pe.wait_ge(sig["expd"], KV * b + kv + 1)
                if kv % KH == 0:
                    if due(2 * b + half - 1):
                        pe.wait_ge(sig["o_free"], 2 * b + half - 1)
                    if kv == 0:
                        pe.wait_ge(sig["vx_ready"], b + 1)
                t.matmul(ps[p0:p0 + VPAD, OB + half, :], vx[:, u, kv, :], pr[:, kv % 2, :],
                         start=True, stop=True).then_inc(sig["pv"], 1)

            steps(pe, step)

            tiles(pe, tile, 1)

        @block.vector
        def _(dve):
            v = nc.vector
            v.memset(zero, 0.0).then_inc(sig["init_zero"], 1)
            v.memset(ones[:, :], 1.0)
            v.memset(qs[:, :, :], 0.0)
            v.memset(ks[:, :, :], 0.0)
            v.memset(mm[:, :, :], 0.0)
            v.memset(kT[:, :, :, :], 0.0)
            v.memset(run[:, 0, :], 0.0).then_inc(sig["const_dve"], 1)
            v.memset(init[:, :, 1:2], 0.0).then_inc(sig["init_add"], 1)
            dve.wait_ge(sig["init_iota"], 1)
            v.tensor_scalar(initi, initi, P - 1, None, ALU.bitwise_and).then_inc(sig["init_and"], 1)
            dve.wait_ge(sig["init_and"], 1)
            v.tensor_scalar(init[:, :, 0:1].rearrange("p r c -> p (r c)"), initi, float(T), None,
                            ALU.add).then_inc(sig["init_add"], 1)

            def x_copy(i, m, r):
                w = r % 2
                dve.wait_ge(sig["x_tr"], i + 1)
                dve.wait_ge(sig["gu"], i - 1 + SH_TILES)
                v.tensor_copy(xT[:, w, :], ps[:, XB, 0:D]).then_inc(sig["xT_ready"], 1)

            def gated(i, m, r, shared):
                w, n = r % 2, nth(i, shared)
                dve.wait_ge(sig["sg_ready"], n)
                if not isinstance(n, int) or n > 2:
                    dve.wait_ge(sig["h_tr"], n - 2)
                v.tensor_tensor(hh[:, w, 0:FF], sg[:, w, :], ps[:, GB + w, FF:GU], ALU.mult).then_inc(sig["h_ready"], 1)

            def tile_list(i):
                gt = oh[:, :, :].rearrange("p k e -> p (k e)").rearrange("p (e k) -> p e k", k=CAP_BLOCKS)
                if i == 2:
                    dve.wait_ge(sig["cnt"], 1)
                    v.tensor_scalar(cc[:, :], ps[:, LB, 0:NEXP], float(CAP), None, ALU.min).then_inc(sig["cc_ready"], 1)
                    dve.wait_ge(sig["cc_ready"], 1)
                    v.tensor_tensor(gt, cc[:, :].unsqueeze(2).broadcast_to([P, NEXP, CAP_BLOCKS]),
                                    thr[:, :].unsqueeze(1).broadcast_to([P, NEXP, CAP_BLOCKS]),
                                    ALU.is_gt).then_inc(sig["gt_ready"], 1)
                if i == 3:
                    dve.wait_ge(sig["gt_ready"], 1)
                    v.tensor_reduce(ntl[:, :], gt, X, ALU.add).then_inc(sig["nt_ready"], 1)
                    dve.wait_ge(sig["nt_ready"], 1)
                    v.tensor_tensor_scan(cum[:, :], ones[:, 0:NEXP], ntl[:, :], 0.0, ALU.mult,
                                         ALU.add).then_inc(sig["cum_ready"], 1)
                if i == 4:
                    dve.wait_ge(sig["cum_ready"], 1)
                    v.tensor_scalar(le[:, 0:NEXP - 1], cum[:, 0:NEXP - 1], jcol[:, :], None,
                                    ALU.is_le).then_inc(sig["le_ready"], 1)
                    dve.wait_ge(sig["le_ready"], 1)
                    v.tensor_reduce(ej[:, :], le[:, 0:NEXP - 1], X, ALU.add).then_inc(sig["ej_ready"], 1)
                if i == 4:
                    v.tensor_tensor(lec[:, 0:NEXP - 1], le[:, 0:NEXP - 1], cum[:, 0:NEXP - 1],
                                    ALU.mult).then_inc(sig["lec_ready"], 1)
                    dve.wait_ge(sig["lec_ready"], 1)
                    v.tensor_reduce(toj[:, :], lec[:, 0:NEXP - 1], X, ALU.max).then_inc(sig["toj_ready"], 1)
                    dve.wait_ge(sig["toj_ready"], 1)
                    v.tensor_tensor(jr[:, :], jcol[:, :], toj[:, :], ALU.subtract).then_inc(sig["jr_ready"], 1)
                    dve.wait_ge(sig["jr_ready"], 1)
                    dve.wait_ge(sig["ej_ready"], 1)
                    v.scalar_tensor_tensor(blk[:, :], ej[:, :], float(CAP_BLOCKS), jr[:, :], ALU.mult,
                                           ALU.add).then_inc(sig["blk_ready"], 1)
                if i == 6:
                    dve.wait_ge(sig["et_mm"], 1)
                    v.tensor_copy(etab[0:1, 0:MOE_TILES], ps[0:1, LB, 0:P]).then_inc(sig["et_ready"], 1)
                if i == 24:
                    dve.wait_ge(sig["idt_tr"], 1)
                    v.tensor_copy(idsT[:, 0:MOE_TILES], ps[:, LB, 0:P]).then_inc(sig["ids_all"], 1)
                    v.tensor_copy(wT[:, 0:MOE_TILES], ps[:, LB, P:2 * P]).then_inc(sig["wt_all"], 1)
                    dve.wait_ge(sig["ids_all"], 1)
                    dve.wait_ge(sig["wt_all"], 1)
                    for k in range(2):
                        v.tensor_copy(ixg[:, k, :], idsT[:, 4 * k:4 * k + 4]).then_inc(sig["ixg_ready"], 1)

            def tile(i, m, r, shared):
                if not shared and r % 4 == 0:
                    if not isinstance(i, int) or i >= 8:
                        for k in range(4):
                            dve.wait_ge(y_st[k], 32 * m + 16 * (r // 4) - 16)
                    v.tensor_copy(ixa[:, r // 4, :], idsT[:, bass.ds(i, 4)]).then_inc(sig["ixa_ready"], 1)
                    v.tensor_copy(wj[:, r // 4, :], wT[:, bass.ds(i, 4)]).then_inc(sig["ixa_ready"], 1)
                nx, nx2 = later(i, m, r, shared, 1), later(i, m, r, shared, 2)
                if nx:
                    gated(*nx)
                if shared and isinstance(i, int):
                    tile_list(i)
                if nx2 and not nx2[3]:
                    x_copy(*nx2[:3])
                if not shared and r % 4 == 3 and (not isinstance(i, int) or i + 5 < MOE_TILES):
                    dve.wait_ge(sig["x_tr"], i + 1)
                    v.tensor_copy(ixg[:, r // 4, :], idsT[:, bass.ds(i + 5, 4)]).then_inc(sig["ixg_ready"], 1)

            def step(b, h, u):
                o = 1 - u

                def rowmax(kv):
                    if has(b, 1):
                        n = KV * (b + 1) + kv
                        if due(n + 1):
                            dve.wait_ge(sig["s1"], n + 1)
                        if kv == 0:
                            if due(b + 1):
                                dve.wait_ge(sig["mm_ready"], b + 1)
                        v.tensor_reduce(nm[:, :, kv], ps[:, SM + kv % 2, :].rearrange("p (g t) -> p g t", g=G),
                                        X, ALU.max, negate=True).then_inc(sig["rowmax"], 1)

                def heads_of(half):
                    return ps[:, OB + half, :].rearrange("p (g k d) -> p k g d", g=G, k=KH)

                def recip(c, half):
                    dve.wait_ge(sig["o_tr"], 2 * c + half + 1)
                    v.reciprocal(den[:, half, :, :, :], heads_of(half)[:, :, :, DH:DH + 1]).then_inc(sig["den_ready"], 1)

                def quotient(c, half):
                    dve.wait_ge(sig["den_ready"], 2 * c + half + 1)
                    v.tensor_tensor(at[:, half * HEADS // 2:(half + 1) * HEADS // 2, :].rearrange("p (k g) d -> p k g d", g=G),
                                    heads_of(half)[:, :, :, 0:DH], den[:, half, :, :, :].broadcast_to([P, KH, G, DH]),
                                    ALU.mult).then_inc(sig["o_free"], 1)

                if isinstance(b, int) and b == 0:
                    dve.wait_ge(sig["const_pool"], NCONST_POOL)
                if isinstance(b, int) and b == B + 1:
                    v.memset(hh[:, 0, FF:D], 0.0).then_inc(sig["h_pad"], 1)
                    gated(0, 0, 0, True)
                    dve.wait_ge(sig["nt_st"], 16 * B)
                    v.memset(hh[:, 1, FF:D], 0.0).then_inc(sig["h_pad"], 1)
                rowmax(0)
                if has(b, -2):
                    c = b - 2
                    dve.wait_ge(sig["tix_ready"], c + 1)
                    v.tensor_copy(ixf[:, :, 0], tix[:, 0:TOPK]).then_inc(sig["ixf_ready"], 1)
                    v.tensor_reduce(s6[:, :], top[:, 0:TOPK], X, ALU.add).then_inc(sig["s6_ready"], 1)
                    dve.wait_ge(sig["ixf_ready"], c + 1)
                    v.tensor_tensor(oh[:, :, :], lane[:, :].unsqueeze(1).broadcast_to([P, TOPK, NEXP]),
                                    ixf[:, :, :].broadcast_to([P, TOPK, NEXP]), ALU.is_equal).then_inc(sig["oh_ready"], 1)
                    dve.wait_ge(sig["s6_ready"], c + 1)
                    v.tensor_scalar(s6e[:, :], s6[:, :], 1e-20, None, ALU.add).then_inc(sig["s6e_ready"], 1)
                if has(b, -1):
                    dve.wait_ge(xr_in[o], 16 * (h + u))
                    if due(16 * (b - 1)):
                        dve.wait_ge(x2_st, 16 * (b - 1))
                rowmax(1)
                if has(b, -2):
                    dve.wait_ge(sig["oh_ready"], c + 1)
                    v.tensor_reduce(mk[:, :], oh[:, :, :].rearrange("p k e -> p e k"), X,
                                    ALU.add).then_inc(sig["mk_ready"], 1)
                    dve.wait_ge(sig["s6e_ready"], c + 1)
                    v.reciprocal(r6[:, :], s6e[:, :]).then_inc(sig["r6_ready"], 1)
                if has(b, -1):
                    recip(b - 1, 1)
                if has(b, -2):
                    dve.wait_ge(sig["mk_ready"], c + 1)
                    v.tensor_tensor(run[:, o, :], run[:, u, :], mk[:, :], ALU.add).then_inc(sig["run_ready"], 1)
                if has(b, -1):
                    quotient(b - 1, 1)
                if has(b, -2):
                    dve.wait_ge(sig["r6_ready"], c + 1)
                    if due(16 * TOPK * (h - 1)):
                        dve.wait_ge(pair_st[u], 16 * TOPK * (h - 1))
                    v.tensor_scalar(dat[:, u, :, 1], top[:, 0:TOPK], r6[:, :], None,
                                    ALU.mult).then_inc(sig["w_ready"], 1)
                if has(b, -1):
                    dve.wait_ge(sig["o_free"], 2 * b)
                    v.tensor_tensor(x2[:, :], at[:, :, :].rearrange("p h d -> p (h d)"), xr[:, o, :],
                                    ALU.add).then_inc(sig["x2_ready"], 1)
                rowmax(2)
                if has(b, -1):
                    dve.wait_ge(sig["x2_ready"], b)
                    v.bn_stats(st2[:, :], x2[:, :]).then_inc(sig["stat2"], 1)
                if has(b, -2):
                    if due(c):
                        dve.wait_ge(sig["tok_ready"], c)
                    v.tensor_copy(dat[:, u, :, 0], tok[:, :].broadcast_to([P, TOPK])).then_inc(sig["ids_ready"], 1)
                if has(b, -1):
                    dve.wait_ge(sig["stat2"], b)
                    if due(b - 1):
                        dve.wait_ge(sig["nb2_ready"], b - 1)
                    settle(dve)
                    v.bn_aggr(mv2[:, :], st2[:, :]).then_inc(sig["mean2"], 1)
                if isinstance(b, int) and b == B + 1:
                    tile(0, 0, 0, True)
                rowmax(3)
                if has(b, 2):
                    dve.wait_ge(sig["qcopy0"], b + 3)
                    if due(b + 2):
                        dve.wait_ge(sig["qs_ready"], b + 2)
                    v.tensor_tensor(rem[:, :, :], n1[:, :, :], qs[:, :, 0:DH], ALU.subtract).then_inc(sig["qrem"], 1)
                if has(b, -2):
                    dve.wait_ge(sig["pos"], c + 1)
                    v.tensor_tensor(pp[:, :, :], oh[:, :, :], ps[:, DB, 0:NEXP].unsqueeze(1).broadcast_to([P, TOPK, NEXP]),
                                    ALU.mult).then_inc(sig["pp_ready"], 1)
                rowmax(4)
                if has(b, -2):
                    dve.wait_ge(sig["pp_ready"], c + 1)
                    v.tensor_reduce(pk[:, :], pp[:, :, :], X, ALU.add).then_inc(sig["pk_ready"], 1)
                    dve.wait_ge(sig["ids_ready"], c + 1)
                    v.tensor_scalar(tok[:, :], tok[:, :], float(P), None, ALU.add).then_inc(sig["tok_ready"], 1)
                    dve.wait_ge(sig["pk_ready"], c + 1)
                    v.tensor_scalar(va[:, :], pk[:, :], float(CAP), None, ALU.is_lt).then_inc(sig["va_ready"], 1)
                    v.scalar_tensor_tensor(sl0[:, :], ixf[:, :, 0], float(CAP), pk[:, :], ALU.mult,
                                           ALU.add).then_inc(sig["sl0_ready"], 1)
                if has(b, 3):
                    dve.wait_ge(xq_in[o], 16 * (h + u + 2))
                    v.bn_stats(st1[:, :], xq[:, o, :]).then_inc(sig["stat1"], 1)
                rowmax(5)
                if has(b, 3):
                    dve.wait_ge(sig["stat1"], b + 4)
                    if due(b + 3):
                        dve.wait_ge(sig["nb1_ready"], b + 3)
                    settle(dve)
                    v.bn_aggr(mv1[:, :], st1[:, :]).then_inc(sig["mean1"], 1)
                if has(b, -2):
                    dve.wait_ge(sig["sl0_ready"], c + 1)
                    if due(c):
                        dve.wait_ge(sig["trc_ready"], c)
                    v.tensor_tensor(sl1[:, :], sl0[:, :], trc[:, :], ALU.subtract).then_inc(sig["sl1_ready"], 1)
                if has(b, 2):
                    dve.wait_ge(sig["qcopy1"], b + 3)
                    v.tensor_tensor(qs[:, :, 5 * DH:6 * DH], rem[:, :, :], qs[:, :, 3 * DH:4 * DH],
                                    ALU.subtract).then_inc(sig["qs_ready"], 1)
                if has(b, -2):
                    dve.wait_ge(sig["sl1_ready"], c + 1)
                    v.tensor_tensor(sl2[:, :], sl1[:, :], va[:, :], ALU.mult).then_inc(sig["sl2_ready"], 1)
                rowmax(6)
                if has(b, -2):
                    dve.wait_ge(sig["sl2_ready"], c + 1)
                    v.tensor_tensor(slot[:, u, :], sl2[:, :], trc[:, :], ALU.add).then_inc(sig["slot_ready"], 1)
                rowmax(7)
                if has(b, -1):
                    dve.wait_ge(sig["lg"], b)
                    v.tensor_reduce(nlm[:, :], ps[:, DB, 0:NEXP], X, ALU.max, negate=True).then_inc(sig["lgmax"], 1)
                if has(b, 1):
                    dve.wait_ge(sig["rowmax"], KV * (b + 2))
                    if due(b + 1):
                        dve.wait_ge(sig["m_tr"], b + 1)
                    mp = mm[:, :, :].rearrange("p g (i r) -> p g i r", i=2)
                    nv = nm[:, :, :].rearrange("p g (k i) -> p g i k", i=2)
                    v.tensor_copy(mp[:, :, :, 0:KV:2], nv).then_inc(sig["mm_hi"], 1)
                if has(b, -2):
                    dve.wait_ge(sig["slot_ready"], c + 1)
                    v.tensor_scalar(trc[:, :], trc[:, :], float(P), None, ALU.add).then_inc(sig["trc_ready"], 1)
                if has(b, 1):
                    dve.wait_ge(sig["mm_hi"], b + 2)
                    v.tensor_tensor(mp[:, :, :, 1:KV:2], nv, mp[:, :, :, 0:KV:2],
                                    ALU.subtract).then_inc(sig["mm_ready"], 1)
                if has(b, 0):
                    recip(b, 0)
                    quotient(b, 0)
                if has(b, -1):
                    dve.wait_ge(sig["pexp"], b)
                    v.reciprocal(rz[:, :], zs[:, :]).then_inc(sig["rz_ready"], 1)
                    dve.wait_ge(sig["rz_ready"], b)
                    v.tensor_scalar(sc[:, :], pe_[:, :], rz[:, :], None, ALU.mult).then_inc(sig["sc_ready"], 1)
                    dve.wait_ge(sig["sc_ready"], b)
                    settle(dve)
                    v.max(top[:, :], sc[:, :]).then_inc(sig["top_ready"], 1)
                    dve.wait_ge(sig["top_ready"], b)
                    settle(dve)
                    v.max_index(tix[:, :], top[:, :], sc[:, :]).then_inc(sig["tix_ready"], 1)

            steps(dve, step)


            tiles(dve, tile, 1)


def kernel(x, ctx_512, L0_ffn_wg_router, L0_ffn_w_gate, L0_ffn_w_up, L0_ffn_w_down,
           L0_ffn_ws_gate, L0_ffn_ws_up, L0_ffn_ws_down):
    import concourse.bacc as bacc
    from concourse.bass_utils import run_bass_kernel_spmd

    def rows(w):
        return w.reshape(w.shape[0], w.shape[1] // P, P, w.shape[2]).transpose(2, 0, 1, 3)

    a = [np.asarray(v) for v in (L0_ffn_w_gate, L0_ffn_w_up, L0_ffn_w_down, L0_ffn_ws_gate, L0_ffn_ws_up, L0_ffn_ws_down)]
    halves = lambda w: w.reshape(D, NSHARED, FF).transpose(1, 0, 2)
    gate = np.concatenate([a[0], halves(a[3])], axis=0)
    up = np.concatenate([a[1], halves(a[4])], axis=0)
    down = np.concatenate([a[2], a[5].reshape(NSHARED, FF, D)], axis=0)
    arrays = {
        "x": np.ascontiguousarray(x),
        "ctx": np.ascontiguousarray(ctx_512),
        "wrT": np.ascontiguousarray(np.asarray(L0_ffn_wg_router).T.reshape(2, P, NEXP).transpose(1, 0, 2)),
        "wgu": np.ascontiguousarray(np.concatenate([rows(gate), rows(up)], axis=3)),
        "wdn0": np.ascontiguousarray(down[:, :F0].transpose(1, 0, 2)),
        "wdn1": np.ascontiguousarray(down[:, F0:].transpose(1, 0, 2)),
    }
    nc = bacc.Bacc("TRN2", target_bir_lowering=False, num_devices=1)
    args = {n: nc.dram_tensor(n, v.shape, mybir.dt.from_np(v.dtype), kind="ExternalInput").ap() for n, v in arrays.items()}
    out = nc.dram_tensor("out", (B, S, D), F32, kind="ExternalOutput").ap()
    build(nc, out=out, **args)
    r = run_bass_kernel_spmd(nc, [arrays], core_ids=[0])
    return r.results[0]["out"]
```
